# Optimizing a Trainium2 kernel written in Bass

```python
import numpy as np
import jax
import jax.numpy as jnp

def _softmax(x, axis=-1):
    return jax.nn.softmax(x, axis=axis)

def _gelu(x):
    return jax.nn.gelu(x, approximate=True)

def _silu(x):
    return jax.nn.silu(x)

def _sigmoid(x):
    return jax.nn.sigmoid(x)

def _layernorm(x, axis=-1, eps=1e-05):
    m = jnp.mean(x, axis=axis, keepdims=True)
    v = jnp.var(x, axis=axis, keepdims=True)
    return (x - m) / jnp.sqrt(v + eps)

def _scatter_add(tgt, idx, src, axis=0):
    return tgt.at[idx].add(src)

def _segment_sum(src, seg, n):
    return jax.ops.segment_sum(src, seg, n)
kernel_name = 'mk_prb_d1_jaxref_r4_de8ee5'

def setup_inputs(seed: int=0):
    np.random.seed(seed)
    _w = jnp.asarray

    def _L0_attn_setup():
        import jax, jax.numpy as jnp
        import numpy as np
        B, S, E, H, D = (1, 512, 256, 16, 64)
        LAM_INIT = 0.8
        LN_EPS = 1e-05
        key = jax.random.key(seed)
        ks = jax.random.split(key, 6)
        w = 0.02
        return {'X': jax.random.normal(ks[0], (B, S, E), dtype=jnp.float32), 'Wq': jax.random.normal(ks[1], (H, E, 2 * D), dtype=jnp.float32) * w, 'bq': jnp.zeros((H, 2 * D), dtype=jnp.float32), 'Wk': jax.random.normal(ks[2], (H, E, 2 * D), dtype=jnp.float32) * w, 'bk': jnp.zeros((H, 2 * D), dtype=jnp.float32), 'Wv': jax.random.normal(ks[3], (H, E, D), dtype=jnp.float32) * w, 'bv': jnp.zeros((H, D), dtype=jnp.float32), 'Wo': jax.random.normal(ks[4], (H * D, E), dtype=jnp.float32) * w, 'bo': jnp.zeros((E,), dtype=jnp.float32), 'gamma': jnp.ones((E,), dtype=jnp.float32), 'beta': jnp.zeros((E,), dtype=jnp.float32), 'lam': jnp.float32(0.5)}
    _L0_attn_in = _L0_attn_setup()

    def _L0_ffn_setup():
        import jax, jax.numpy as jnp
        import numpy as np
        B, S, D = (4, 512, 256)
        E, F = (8, 1024)
        key = jax.random.key(seed)
        ks = jax.random.split(key, 5)
        x = jax.random.normal(ks[0], (B, S, D), dtype=jnp.float32)
        switch_w = jax.random.normal(ks[1], (D, E), dtype=jnp.float32) * D ** (-0.5)
        switch_b = jnp.zeros((E,), dtype=jnp.float32)
        w1 = jax.random.normal(ks[2], (E, D, F), dtype=jnp.float32) * D ** (-0.5)
        b1 = jnp.zeros((E, F), dtype=jnp.float32)
        w2 = jax.random.normal(ks[3], (E, F, D), dtype=jnp.float32) * F ** (-0.5)
        b2 = jnp.zeros((E, D), dtype=jnp.float32)
        return {'x': x, 'switch_w': switch_w, 'switch_b': switch_b, 'w1': w1, 'b1': b1, 'w2': w2, 'b2': b2}
    _L0_ffn_in = _L0_ffn_setup()
    _d = {'L0_attn_X': _L0_attn_in['X'], 'L0_attn_Wq': _L0_attn_in['Wq'], 'L0_attn_bq': _L0_attn_in['bq'], 'L0_attn_Wk': _L0_attn_in['Wk'], 'L0_attn_bk': _L0_attn_in['bk'], 'L0_attn_Wv': _L0_attn_in['Wv'], 'L0_attn_bv': _L0_attn_in['bv'], 'L0_attn_Wo': _L0_attn_in['Wo'], 'L0_attn_bo': _L0_attn_in['bo'], 'L0_attn_gamma': _L0_attn_in['gamma'], 'L0_attn_beta': _L0_attn_in['beta'], 'L0_attn_lam': _L0_attn_in['lam'], 'L0_ffn_switch_w': _L0_ffn_in['switch_w'], 'L0_ffn_switch_b': _L0_ffn_in['switch_b'], 'L0_ffn_w1': _L0_ffn_in['w1'], 'L0_ffn_b1': _L0_ffn_in['b1'], 'L0_ffn_w2': _L0_ffn_in['w2'], 'L0_ffn_b2': _L0_ffn_in['b2']}
    _x0 = _d['L0_attn_X']
    _d['L0_attn_X'] = jax.random.normal(jax.random.fold_in(jax.random.key(seed), 1), (8, 512, 256), dtype=_x0.dtype)
    del _x0
    return _d

def reference(L0_attn_X, L0_attn_Wq, L0_attn_bq, L0_attn_Wk, L0_attn_bk, L0_attn_Wv, L0_attn_bv, L0_attn_Wo, L0_attn_bo, L0_attn_gamma, L0_attn_beta, L0_attn_lam, L0_ffn_switch_w, L0_ffn_switch_b, L0_ffn_w1, L0_ffn_b1, L0_ffn_w2, L0_ffn_b2):

    def _L0_attn_ref(X, Wq, bq, Wk, bk, Wv, bv, Wo, bo, gamma, beta, lam):
        import jax, jax.numpy as jnp
        import numpy as np
        B, S, E, H, D = (1, 512, 256, 16, 64)
        LAM_INIT = 0.8
        LN_EPS = 1e-05
        Q = jnp.einsum('bse,hec->bhsc', X, Wq) + bq[None, :, None, :]
        K = jnp.einsum('bse,hec->bhsc', X, Wk) + bk[None, :, None, :]
        V = jnp.einsum('bse,hed->bhsd', X, Wv) + bv[None, :, None, :]
        d = Wv.shape[-1]
        Q1, Q2 = (Q[..., :d], Q[..., d:])
        K1, K2 = (K[..., :d], K[..., d:])
        s = 1.0 / jnp.sqrt(jnp.float32(d))
        A1 = jnp.einsum('bhqd,bhkd->bhqk', Q1, K1) * s
        A2 = jnp.einsum('bhqd,bhkd->bhqk', Q2, K2) * s
        P = jax.nn.softmax(A1, axis=-1) - lam * jax.nn.softmax(A2, axis=-1)
        O = jnp.einsum('bhqk,bhkd->bhqd', P, V)
        Ocat = jnp.transpose(O, (0, 2, 1, 3)).reshape(O.shape[0], O.shape[2], -1)
        Y = Ocat @ Wo + bo
        mu = jnp.mean(Y, axis=-1, keepdims=True)
        var = jnp.var(Y, axis=-1, keepdims=True)
        Yn = (Y - mu) * jax.lax.rsqrt(var + LN_EPS) * gamma + beta
        return Yn * (1.0 - LAM_INIT)

    def _L0_ffn_ref(x, switch_w, switch_b, w1, b1, w2, b2):
        import jax, jax.numpy as jnp
        import numpy as np
        B, S, D = (4, 512, 256)
        E, F = (8, 1024)
        b, s, d = x.shape
        t = x.reshape(-1, d)
        logits = t @ switch_w + switch_b
        route_prob = jax.nn.softmax(logits, axis=-1)
        route_prob_max = jnp.max(route_prob, axis=-1)
        routes = jnp.argmax(route_prob, axis=-1)
        out = jnp.zeros_like(t)
        n_experts = w1.shape[0]
        for e in range(n_experts):
            h = jax.nn.gelu(t @ w1[e] + b1[e])
            y = h @ w2[e] + b2[e]
            mask = (routes == e)[:, None]
            out = jnp.where(mask, y, out)
        out = out * route_prob_max[:, None]
        return out.reshape(b, s, d)
    x = L0_attn_X
    xn = _layernorm(x, axis=-1)
    x = x + _L0_attn_ref(xn, L0_attn_Wq, L0_attn_bq, L0_attn_Wk, L0_attn_bk, L0_attn_Wv, L0_attn_bv, L0_attn_Wo, L0_attn_bo, L0_attn_gamma, L0_attn_beta, L0_attn_lam) + _L0_ffn_ref(xn, L0_ffn_switch_w, L0_ffn_switch_b, L0_ffn_w1, L0_ffn_b1, L0_ffn_w2, L0_ffn_b2)
    return x

_drawn_inputs = setup_inputs


def setup_inputs(seed=0):
    import zlib

    import numpy as np

    out = dict(_drawn_inputs(seed))
    spreads = {'L0_attn_bq': (0.0, 0.8),
     'L0_attn_bk': (0.0, 2.0),
     'L0_attn_bv': (0.0, 0.8),
     'L0_attn_bo': (0.0, 0.432),
     'L0_attn_gamma': (1.0, 0.2),
     'L0_attn_beta': (0.0, 0.464),
     'L0_ffn_switch_b': (0.0, 0.1),
     'L0_ffn_b1': (0.0, 0.309),
     'L0_ffn_b2': (0.0, 0.1)}
    factors = {'L0_attn_Wq': 8.0, 'L0_attn_Wk': 8.0, 'L0_attn_Wv': 5.894}
    for name, (base, spread) in spreads.items():
        noise = np.random.default_rng([zlib.crc32(name.encode()), seed]).standard_normal(out[name].shape)
        drawn = base * np.exp(spread * noise) if base else spread * noise
        out[name] = jnp.asarray(drawn.astype(out[name].dtype))
    for name, factor in factors.items():
        out[name] = (out[name] * factor).astype(out[name].dtype)
    return out
```

```python
from contextlib import ExitStack

import concourse.bass as bass
from concourse import mybir

F32 = mybir.dt.float32
F32R = mybir.dt.float32r
I32 = mybir.dt.int32
U32 = mybir.dt.uint32
ALU = mybir.AluOpType
ACT = mybir.ActivationFunctionType
AXX = mybir.AxisListType.X

P = 128
B, S, E = 8, 512, 256
H, D = 16, 64
T = B * S
NT = T // P
KT = E // P
EPS = 1e-5
OUT_SCALE = 1.0 - 0.8
NE, F = 8, 1024
FT = F // P
FFN_TILE = 256
FFN_TILES = (T + NE * (FFN_TILE - 1)) // FFN_TILE
SLOTS = FFN_TILES * FFN_TILE
FS = FFN_TILE // P
MAXT = T // FFN_TILE
PAIRS = H // 2
QT = S // P
TPP = 2 * QT
ITERS = B * PAIRS // 2
WPAIR = KT * (2 * P + 2 * P + 2 * D)
C_ID, C_UP, C_J, C_T = 0, P, 2 * P, 2 * P + MAXT
CONSTS = C_T + FFN_TILES


def looped(engine, count, body, peel_last=False):
    body(0, True, False)
    end = count - 1 if peel_last else count
    with engine.Fori(1, end) as turn:
        body(turn, False, False)
    if peel_last:
        body(count - 1, False, True)


MOMENT_STEPS, RECIPROCAL_STEP = 9, 5


def moments(nc, dve, step, stats, mom, s_root, roots):
    v = nc.vector
    mean, rstd, dif, ve, rec, root = (mom[:, k, :] for k in range(6))
    v.tensor_tensor(mean, stats[:, :, 1], stats[:, :, 4], ALU.add)
    v.tensor_tensor(dif, stats[:, :, 1], stats[:, :, 4], ALU.subtract)
    step(v.tensor_tensor(ve, stats[:, :, 2], stats[:, :, 5], ALU.add))
    v.tensor_scalar(mean, mean, 0.5, None, ALU.mult)
    v.tensor_scalar(dif, dif, 0.5, None, ALU.mult)
    step(v.tensor_scalar(ve, ve, 1.0 / E, EPS, ALU.mult, ALU.add))
    step(v.tensor_tensor(dif, dif, dif, ALU.mult))
    step(v.tensor_tensor(ve, ve, dif, ALU.add))
    step(v.reciprocal(rec, ve))
    dve.wait_ge(s_root, roots)
    step(v.tensor_tensor(dif, root, root, ALU.mult))
    step(v.tensor_tensor(dif, dif, ve, ALU.mult))
    step(v.tensor_scalar(dif, dif, -0.5, 1.5, ALU.mult, ALU.add))
    step(v.tensor_tensor(rstd, root, dif, ALU.mult))


def norm_stage(nc, ins, xn_d, xs_d, xT, consts, sw, pL):
    G = 2 * P
    TURN = 4
    TURNS = T // G // TURN
    with ExitStack() as ctx:
        def sb(name, shape, dt=F32):
            return ctx.enter_context(nc.sbuf_tensor(name, shape, dt))

        def sem(name):
            return ctx.enter_context(nc.semaphore(name))

        xin = [sb(f"xin{j}", [P, 2, E]) for j in range(TURN)]
        xn = [sb(f"xn{j}", [P, 2, E]) for j in range(TURN)]
        xt = [sb(f"xt{a}", [P, KT, G]) for a in range(2)]
        stats, mom = sb("stats", [P, 2 * TURN, 6]), sb("mom", [P, 6, 2 * TURN])
        ZC = SLOTS * E // P // 8
        zeros = sb("zeros", [P, ZC])
        pX = [ctx.enter_context(nc.psum_tensor(f"pX{a}", [P, KT, G], F32)) for a in range(2)]
        s_const, s_zero, s_zeroed = sem("n_const"), sem("n_zero"), sem("n_zeroed")
        s_x = [sem(f"n_x{j}") for j in range(TURN)]
        s_store = [sem(f"n_store{j}") for j in range(TURN)]
        s_xT = [sem(f"n_xT{a}") for a in range(2)]
        s_stat, s_d, s_root, s_xn = sem("n_stat"), sem("n_dve"), sem("n_root"), sem("n_xn")
        s_tr, s_xt, s_logit = sem("n_tr"), sem("n_xt"), sem("n_logit")
        x_d = ins["x"].rearrange("(n s p) e -> n p s e", s=2, p=P)
        xn_v = xn_d.rearrange("(n s p) e -> n p s e", s=2, p=P)

        def at(ap, n):
            return ap[bass.ds(n, 1)].rearrange("a p s e -> (a p) s e")

        block = ctx.enter_context(nc.Block())

        @block.sync
        def _(sp):
            for j in range(TURN):
                sp.dma_start(xin[j][:, :, :], at(x_d, j)).then_inc(s_x[j], 16)
            sp.dma_start(consts[:, :], ins["consts"]).then_inc(s_const, 16)
            sp.dma_start(sw[:, :, :], ins["sw"]).then_inc(s_const, 16)

            def body(i, first, last):
                for j in range(TURN):
                    n = TURN * i + j
                    sp.wait_ge(s_xn, n + 1)
                    if not last:
                        sp.dma_start(xin[j][:, :, :], at(x_d, n + TURN)).then_inc(s_x[j], 16)
                    sp.dma_start(at(xn_v, n), xn[j][:, :, :]).then_inc(s_store[j], 16)
            looped(sp, TURNS, body, peel_last=True)
            sp.wait_ge(s_zero, 1)
            zv = xs_d.rearrange("(c q) e -> c (q e)", c=8).rearrange("c (p n) -> c p n", p=P)
            for c in range(8):
                sp.dma_start(zv[c], zeros[:, :]).then_inc(s_zeroed, 16)
            for j in range(TURN):
                sp.wait_ge(s_store[j], 16 * TURNS)
            sp.wait_ge(s_zeroed, 16 * 8)

        @block.gpsimd
        def _(pool):
            nc.gpsimd.memset(zeros[:, :], 0.0).then_inc(s_zero, 1)

        @block.vector
        def _(dve):
            def body(i, first, last):
                done = [0]

                def step(ins_):
                    done[0] += 1
                    ins_.then_inc(s_d, 1)
                    dve.wait_ge(s_d, MOMENT_STEPS * i + done[0])

                for j in range(TURN):
                    dve.wait_ge(s_x[j], 16 * (i + 1))
                    for s in range(2):
                        nc.vector.bn_stats(stats[:, 2 * j + s, :], xin[j][:, s, :]).then_inc(s_stat, 1)
                dve.wait_ge(s_stat, 2 * TURN * (i + 1))
                moments(nc, dve, step, stats, mom, s_root, i + 1)
                for j in range(TURN):
                    n = TURN * i + j
                    if not first:
                        dve.wait_ge(s_tr, n - TURN + 1)
                        dve.wait_ge(s_store[j], 16 * i)
                    for s in range(2):
                        a = 2 * j + s
                        last_op = nc.vector.tensor_scalar(xn[j][:, s, :], xin[j][:, s, :], mom[:, 0, a:a + 1],
                                                          mom[:, 1, a:a + 1], ALU.subtract, ALU.mult)
                    last_op.then_inc(s_xn, 1)
            looped(dve, TURNS, body)

        @block.scalar
        def _(act):
            def root(i):
                act.wait_ge(s_d, MOMENT_STEPS * i + RECIPROCAL_STEP)
                nc.scalar.activation(mom[:, 5, :], mom[:, 4, :], ACT.Sqrt).then_inc(s_root, 1)

            def body(i, first, last):
                for j in range(TURN):
                    n, a = TURN * i + j, j % 2
                    act.wait_ge(s_tr, n + 1)
                    if not (first and j < 2):
                        act.wait_ge(s_logit, n - 1)
                        act.wait_ge(s_xT[a], 16 * ((TURN // 2) * i + j // 2))
                    nc.scalar.copy(xt[a][:, :, :], pX[a][:, :, :]).then_inc(s_xt, 1)
                    act.wait_ge(s_xt, n + 1)
                    act.dma_start(xT[:, :, bass.ds(n * G, G)], xt[a][:, :, :]).then_inc(s_xT[a], 16)
                    if j == 1 and not last:
                        root(i + 1)
            root(0)
            looped(act, TURNS, body, peel_last=True)
            for a in range(2):
                act.wait_ge(s_xT[a], 16 * TURNS * TURN // 2)

        @block.tensor
        def _(pe):
            pe.wait_ge(s_const, 32)
            ident = consts[:, C_ID:C_ID + P]

            def body(i, first, last):
                for j in range(TURN):
                    n, a = TURN * i + j, j % 2
                    pe.wait_ge(s_xn, n + 1)
                    if not (first and j < 2):
                        pe.wait_ge(s_xt, n - 1)
                    for k in range(KT):
                        for s in range(2):
                            last_op = nc.tensor.transpose(pX[a][:, k, s * P:(s + 1) * P],
                                                          xn[j][:, s, k * P:(k + 1) * P], ident)
                    last_op.then_inc(s_tr, 1)
                    if not (first and j == 0):
                        logits(n - 1, 1 - a)

            def logits(n, a):
                pe.wait_ge(s_xt, n + 1)
                for s in range(2):
                    for k in range(KT):
                        last_op = nc.tensor.matmul(pL[:, bass.ds((n * 2 + s) * NE, NE)],
                                                   xt[a][:, k, s * P:(s + 1) * P], sw[:, k, :],
                                                   start=(k == 0), stop=(k == KT - 1))
                last_op.then_inc(s_logit, 1)

            looped(pe, TURNS, body)
            logits(TURNS * TURN - 1, 1)


def route_stage(nc, ins, consts, pL, slot_u, prob, tile_expert):
    with ExitStack() as ctx:
        def sb(name, shape, dt=F32):
            return ctx.enter_context(nc.sbuf_tensor(name, shape, dt))

        def sem(name):
            return ctx.enter_context(nc.semaphore(name))

        swb, weight = sb("swb", [P, NE]), sb("weight", [P, NE])
        lg, ex, oh = sb("lg", [P, NT, NE]), sb("ex", [P, NT, NE]), sb("oh", [P, NT, NE])
        col, den = sb("col", [P, NT]), sb("den", [P, NT])
        inc, exc = sb("inc", [P, NE, NT]), sb("exc", [P, NE, NT])
        ones, upper = sb("ones", [P, P]), consts[:, C_UP:C_UP + P]
        more = sb("more", [P, NE, MAXT])
        tiles, tile_end, base = sb("tiles", [P, NE]), sb("tile_end", [P, NE]), sb("base", [P, NE])
        slot_f = sb("slot_f", [P, NT])
        past, te_f = sb("past", [P, FFN_TILES, NE]), sb("te_f", [P, FFN_TILES])
        pR = ctx.enter_context(nc.psum_tensor("pR", [P, NT, NE], F32))
        pC = ctx.enter_context(nc.psum_tensor("pC", [P, NT, NE], F32))
        s_in, s_d, s_e, s_rank, s_p = sem("r_in"), sem("r_dve"), sem("r_exp"), sem("r_rank"), sem("r_pool")
        block = ctx.enter_context(nc.Block())
        SHIFTED, ONEHOT = 3, 9

        @block.sync
        def _(sp):
            sp.dma_start(swb[:, :], ins["swb"]).then_inc(s_in, 16)

        @block.gpsimd
        def _(pool):
            nc.gpsimd.memset(ones[:, :], 1.0).then_inc(s_p, 1)
            for e in range(NE):
                last_op = nc.gpsimd.memset(weight[:, e:e + 1], float(NE - e))
            last_op.then_inc(s_p, 1)

        @block.scalar
        def _(act):
            act.wait_ge(s_d, SHIFTED)
            nc.scalar.activation(ex[:, :, :], lg[:, :, :], ACT.Exp).then_inc(s_e, 1)

        @block.tensor
        def _(pe):
            pe.wait_ge(s_p, 2)
            pe.wait_ge(s_d, ONEHOT)
            nc.tensor.matmul(pR[:, :, :], upper, oh[:, :, :], start=True, stop=True)
            nc.tensor.matmul(pC[:, :, :], ones[:, :], oh[:, :, :], start=True, stop=True).then_inc(s_rank, 1)

        @block.vector
        def _(dve):
            done = [0]

            def step(ins_):
                done[0] += 1
                ins_.then_inc(s_d, 1)
                dve.wait_ge(s_d, done[0])

            tne, v = [P, NT, NE], nc.vector
            pLv = pL[:, 0:NT * NE].rearrange("p (t e) -> p t e", e=NE)
            dve.wait_ge(s_in, 16)
            step(v.tensor_tensor(lg[:, :, :], pLv, swb[:, :].unsqueeze(1).to_broadcast(tne), ALU.add))
            step(v.tensor_reduce(col[:, :], lg[:, :, :], AXX, ALU.max))
            step(v.tensor_tensor(lg[:, :, :], lg[:, :, :], col[:, :].unsqueeze(2).to_broadcast(tne), ALU.subtract))
            dve.wait_ge(s_p, 2)
            dve.wait_ge(s_e, 1)
            step(v.tensor_reduce(den[:, :], ex[:, :, :], AXX, ALU.add))
            step(v.reciprocal(prob[:, :], den[:, :]))
            step(v.tensor_scalar(oh[:, :, :], lg[:, :, :], 0.0, None, ALU.is_equal))
            step(v.tensor_tensor(ex[:, :, :], oh[:, :, :], weight[:, :].unsqueeze(1).to_broadcast(tne), ALU.mult))
            step(v.tensor_reduce(col[:, :], ex[:, :, :], AXX, ALU.max))
            step(v.tensor_tensor(oh[:, :, :], ex[:, :, :], col[:, :].unsqueeze(2).to_broadcast(tne), ALU.is_equal))
            dve.wait_ge(s_rank, 1)
            cnt = pC[:, :, :].rearrange("p t e -> p e t")
            for e in range(NE):
                last_op = v.tensor_tensor_scan(inc[:, e, :], ones[:, 0:NT], cnt[:, e, :], 0.0, ALU.mult, ALU.add)
            step(last_op)
            step(v.tensor_tensor(exc[:, :, :], inc[:, :, :], cnt, ALU.subtract))
            em = [P, NE, MAXT]
            step(v.tensor_tensor(more[:, :, :], inc[:, :, NT - 1:NT].to_broadcast(em),
                                 consts[:, C_J:C_J + MAXT].unsqueeze(1).to_broadcast(em), ALU.is_gt))
            step(v.tensor_reduce(tiles[:, :], more[:, :, :], AXX, ALU.add))
            step(v.tensor_tensor_scan(tile_end[:, :], ones[:, 0:NE], tiles[:, :], 0.0, ALU.mult, ALU.add))
            step(v.tensor_tensor(base[:, :], tile_end[:, :], tiles[:, :], ALU.subtract))
            step(v.tensor_scalar(base[:, :], base[:, :], float(FFN_TILE), None, ALU.mult))
            step(v.tensor_tensor(lg[:, :, :], pR[:, :, :], exc[:, :, :].rearrange("p e t -> p t e"), ALU.add))
            step(v.tensor_tensor(lg[:, :, :], lg[:, :, :], base[:, :].unsqueeze(1).to_broadcast(tne), ALU.add))
            step(v.tensor_tensor(lg[:, :, :], lg[:, :, :], oh[:, :, :], ALU.mult))
            step(v.tensor_reduce(slot_f[:, :], lg[:, :, :], AXX, ALU.add))
            step(v.tensor_copy(slot_u[:, :], slot_f[:, :]))
            fe = [P, FFN_TILES, NE]
            step(v.tensor_tensor(past[:, :, :], tile_end[:, :].unsqueeze(1).to_broadcast(fe),
                                 consts[:, C_T:C_T + FFN_TILES].unsqueeze(2).to_broadcast(fe), ALU.is_le))
            step(v.tensor_reduce(te_f[:, :], past[:, :, :], AXX, ALU.add))
            step(v.tensor_scalar(te_f[:, :], te_f[:, :], float(NE - 1), None, ALU.min))
            step(v.tensor_copy(tile_expert[:, :], te_f[:, :]))


def attention_stage(nc, ins, xn_d, xs_d, oT_d, xT, consts, slot_u):
    SCALE = float(D) ** -0.5
    with ExitStack() as ctx:
        def sb(name, shape, dt=F32):
            return ctx.enter_context(nc.sbuf_tensor(name, shape, dt))

        def ps(name, shape):
            return ctx.enter_context(nc.psum_tensor(name, shape, F32))

        def sem(name):
            return ctx.enter_context(nc.semaphore(name))

        w = [sb(f"w{j}", [P, WPAIR]) for j in range(2)]
        bias = sb("bias", [P, 2 * H + PAIRS])
        lam = sb("lam", [P, 1])
        parts = {"q": [sb(f"q_parts{u}", [P, 2, S], F32R) for u in range(2)],
                 "k": [sb(f"k_parts{u}", [P, 2, S], F32R) for u in range(2)]}
        qs = [[sb(f"qs{j}{u}", [P, 2, S], F32R) for u in range(2)] for j in range(2)]
        ks = [[sb(f"ks{j}{u}", [P, 2, 2, S], F32R) for u in range(2)] for j in range(2)]
        vT = sb("vT", [P, S])
        v = [sb(f"v{j}", [P, QT, P]) for j in range(2)]
        ex = sb("e", [P, 4, 2, S])
        pm = sb("pm", [P, 4, S])
        pT = [[sb(f"pT{j}{u}", [P, QT, S]) for u in range(2)] for j in range(2)]
        oT = [sb(f"oT{j}", [P, S]) for j in range(2)]
        nmax, nbias = sb("nmax", [P, 2, 2]), sb("nbias", [P, 2, 2])
        rsum, rrec, coef = sb("rsum", [P, 4, 2]), sb("rrec", [P, 4, 2]), sb("coef", [P, 4, 1])
        row, row_slot = sb("row", [P, E]), sb("row_slot", [P, 1], U32)
        p_score = [ps(f"p_score{a}", [P, 2, S]) for a in range(2)]
        p_tr, p_pv = ps("p_tr", [P, QT, P]), ps("p_pv", [P, S])
        p_proj = [ps(f"p_proj{a}", [P, S]) for a in range(2)]

        s_const, s_w, s_dup = sem("a_const"), [sem(f"a_w{j}") for j in range(2)], \
            [[sem(f"a_dup{j}{u}") for u in range(2)] for j in range(2)]
        s_proj, s_hi, s_lo, s_vT, s_v = sem("a_proj"), sem("a_hi"), sem("a_lo"), sem("a_vT"), sem("a_v")
        s_score, s_max, s_nbias, s_exp = sem("a_score"), sem("a_max"), sem("a_nbias"), sem("a_exp")
        s_rec, s_coef, s_e1, s_comb = sem("a_rec"), sem("a_coef"), sem("a_e1"), sem("a_comb")
        s_tr, s_pT, s_pv, s_o = sem("a_tr"), sem("a_pT"), sem("a_pv"), sem("a_o")
        s_ost = [sem(f"a_ost{j}") for j in range(2)]
        s_row, s_idx, s_scat, s_lam = sem("a_row"), sem("a_idx"), sem("a_scat"), sem("a_lam")

        w_d = ins["w_attn"]
        ident = consts[:, C_ID:C_ID + P]
        LAG = 4
        DUPS = 8

        ORDER = ("q0", "k0", "q1", "k1", "v", "vt")
        AT_STEP = {0: "q0", 1: "k0", 2: "q1", 3: "k1", 4: "v", 5: "vt"}
        PV_STEP = {5: (0,), 6: (1, 2), 7: (3,)}

        def batch_of(pair):
            return pair // PAIRS

        def weights(j, what, u, k):
            if what == "v":
                return w[j][:, KT * 4 * P + k * P:KT * 4 * P + (k + 1) * P]
            o = (0 if what == "q" else KT * 2 * P) + k * 2 * P + u * P
            return w[j][:, o:o + P]

        block = ctx.enter_context(nc.Block())

        @block.sync
        def _(sp):
            sp.dma_start(bias[:, :], ins["attn_bias"]).then_inc(s_const, 16)
            sp.dma_start(lam[:, :], ins["lam"]).then_inc(s_const, 16)
            for j in range(2):
                sp.nop().then_inc(s_ost[j], 16)

            def load_w(pair, j):
                src = w_d[bass.ds(pair % PAIRS, 1)].rearrange("a p n -> (a p) n")
                sp.dma_start(w[j][:, :], src).then_inc(s_w[j], 16)

            def spread(j, u, what, pair):
                n = 4 * pair + 2 * u + (what == "k")
                sp.wait_ge(s_lo, n + 1)
                src = parts[what][u]
                for m in range(2):
                    a = src[m * D:(m + 1) * D]
                    if what == "q":
                        for part in range(2):
                            sp.dma_start(qs[j][u][part * D:(part + 1) * D, m, :].bitcast(F32),
                                         a[:, part, :].bitcast(F32)).then_inc(s_dup[j][u], 16)
                    else:
                        for half in range(2):
                            sp.dma_start(ks[j][u][half * D:(half + 1) * D, m, :, :].bitcast(F32),
                                         a[:, :, :].bitcast(F32)).then_inc(s_dup[j][u], 16)

            load_w(0, 0)
            load_w(1, 1)
            for u in range(2):
                for what in "qk":
                    spread(0, u, what, 0)

            def body(it, first, last):
                if not first:
                    sp.wait_ge(s_scat, 16 * it)
                sp.dma_start(row[:, :], xn_d[bass.ds(it * P, P), :]).then_inc(s_row, 16)
                for j in range(2):
                    pair = 2 * it + j
                    nj = 1 - j
                    if not last:
                        sp.wait_ge(s_proj, 6 * pair + 5)
                        load_w(pair + 2, j)
                    if not (last and j == 1):
                        for u in range(2):
                            for what in "qk":
                                spread(nj, u, what, pair + 1)
                    if not first:
                        store_o(pair - 2, j)

            def store_o(pair, j):
                sp.wait_ge(s_o, pair + 1)
                dst = oT_d[bass.ds(pair % PAIRS, 1), :, bass.ds(batch_of(pair) * S, S)]
                sp.dma_start(dst.rearrange("a p n -> (a p) n"), oT[j][:, :]).then_inc(s_ost[j], 16)

            looped(sp, ITERS, body, peel_last=True)
            store_o(2 * ITERS - 2, 0)
            store_o(2 * ITERS - 1, 1)
            for j in range(2):
                sp.wait_ge(s_ost[j], 16 * (ITERS + 1))

        @block.gpsimd
        def _(pool):
            def body(it, first, last):
                if not first:
                    pool.wait_ge(s_scat, 16 * it)
                nc.gpsimd.tensor_copy(row_slot[:, :], slot_u[:, bass.ds(it, 1)]).then_inc(s_idx, 1)
                for t in range(2 * TPP):
                    g = it * 2 * TPP + t
                    if t == 2:
                        pool.wait_ge(s_row, 16 * (it + 1))
                        pool.wait_ge(s_idx, it + 1)
                    pool.wait_ge(s_rec, g + 1)
                    e1 = ex[:, t % 4, 0, :]
                    nc.gpsimd.tensor_tensor(e1, e1, rrec[:, t % 4, 0:1].to_broadcast([P, S]), ALU.mult
                                            ).then_inc(s_e1, 1)
                    if t == 2:
                        pool.indirect_dma_start(
                            out=xs_d, out_offset=bass.IndirectOffsetOnAxis(ap=row_slot[:, 0:1], axis=0),
                            in_=row[:, :], in_offset=None).then_inc(s_scat, 16)
            looped(pool, ITERS, body, peel_last=True)
            pool.wait_ge(s_scat, 16 * ITERS)

        @block.scalar
        def _(act):
            act.wait_ge(s_const, 32)

            def high_part(pair, j, u, what, fresh=False):
                n = 4 * pair + 2 * u + (what == "k")
                act.wait_ge(s_proj, 6 * pair + ORDER.index(f"{what}{u}") + 1)
                if not fresh:
                    act.wait_ge(s_dup[1 - j][u], 16 * DUPS * ((pair - 1) // 2 + 1))
                b = bias[:, bass.ds((pair % PAIRS) * 2 + (0 if what == "q" else H) + u, 1)]
                nc.scalar.activation(parts[what][u][:, 0, :], p_proj[n % 2][:, :],
                                     ACT.Identity, bias=b).then_inc(s_hi, 1)

            def v_bias(pair):
                act.wait_ge(s_proj, 6 * pair + 5)
                b = bias[:, bass.ds(2 * H + pair % PAIRS, 1)]
                nc.scalar.activation(vT[:, :], p_proj[0][:, :], ACT.Identity, bias=b).then_inc(s_vT, 1)

            def copy_pT(g, j, u, qt, pair, fresh):
                act.wait_ge(s_tr, g + 1)
                if u == qt == 0 and not fresh:
                    act.wait_ge(s_pv, pair - 1)
                nc.scalar.copy(pT[j][u][:, :, qt * P:(qt + 1) * P], p_tr[:, :, :]).then_inc(s_pT, 1)

            for n, what in enumerate(ORDER[:4]):
                high_part(0, 0, n // 2, what[0], True)
            v_bias(0)

            def body(it, first, last):
                for t in range(2 * TPP):
                    j, st = t // TPP, t % TPP
                    g, pair = it * 2 * TPP + t, 2 * it + j
                    if not (first and t < LAG):
                        lt = (t - LAG) % (2 * TPP)
                        lj, lst = lt // TPP, lt % TPP
                        lpair = pair if t % TPP >= LAG else pair - 1
                        copy_pT(g - LAG, lj, lst // QT, lst % QT, lpair, first)
                    what = AT_STEP.get(st - 1)
                    if what and not (last and j == 1):
                        if what[0] in "qk":
                            high_part(pair + 1, 1 - j, int(what[1]), what[0])
                        elif what == "v":
                            v_bias(pair + 1)
                    for m in range(2):
                        act.wait_ge(s_nbias, g + 1)
                        if m == 0 and not (first and t < 4):
                            act.wait_ge(s_comb, g - 3)
                        nc.scalar.activation(ex[:, t % 4, m, :], p_score[t % 2][:, m, :], ACT.Exp,
                                             bias=nbias[:, t % 2, m:m + 1], scale=SCALE,
                                             accum_out=rsum[:, t % 4, m:m + 1]).then_inc(s_exp, 1)
            looped(act, ITERS, body, peel_last=True)
            g = ITERS * 2 * TPP
            for t in range(LAG):
                lst = TPP - LAG + t
                copy_pT(g - LAG + t, 1, lst // QT, lst % QT, 2 * ITERS - 1, False)

        @block.vector
        def _(dve):
            dve.wait_ge(s_const, 32)
            nc.vector.tensor_scalar(lam[:, :], lam[:, :], -1.0, None, ALU.mult).then_inc(s_lam, 1)
            dve.wait_ge(s_lam, 1)

            def low_part(pair, j, u, what):
                n = 4 * pair + 2 * u + (what == "k")
                dve.wait_ge(s_hi, n + 1)
                b = bias[:, bass.ds((pair % PAIRS) * 2 + (0 if what == "q" else H) + u, 1)]
                nc.vector.scalar_tensor_tensor(out=parts[what][u][:, 1, :], in0=p_proj[n % 2][:, :], scalar=b,
                                               in1=parts[what][u][:, 0, :].bitcast(F32),
                                               op0=ALU.add, op1=ALU.subtract).then_inc(s_lo, 1)

            def copy_v(pair, j, fresh):
                dve.wait_ge(s_proj, 6 * pair + 6)
                if not fresh:
                    dve.wait_ge(s_pv, pair - 1)
                nc.vector.tensor_copy(v[j][:, :, :], p_proj[1][:, :].rearrange("p (k d) -> p k d", d=P)
                                      ).then_inc(s_v, 1)

            def copy_o(pair, j):
                dve.wait_ge(s_pv, pair + 1)
                dve.wait_ge(s_ost[j], 16 * (pair // 2 + 1))
                nc.vector.tensor_copy(oT[j][:, :], p_pv[:, :]).then_inc(s_o, 1)

            def reciprocals(g, b):
                dve.wait_ge(s_exp, 2 * g + 2)
                nc.vector.reciprocal(rrec[:, b, :], rsum[:, b, :]).then_inc(s_rec, 1)
                dve.wait_ge(s_rec, g + 1)
                nc.vector.tensor_tensor(coef[:, b, :], rrec[:, b, 1:2], lam[:, :], ALU.mult).then_inc(s_coef, 1)

            def combine(g, b, fresh):
                dve.wait_ge(s_e1, g + 1)
                dve.wait_ge(s_coef, g + 1)
                if not fresh:
                    dve.wait_ge(s_tr, g - 3)
                nc.vector.scalar_tensor_tensor(out=pm[:, b, :], in0=ex[:, b, 1, :], scalar=coef[:, b, :],
                                               in1=ex[:, b, 0, :], op0=ALU.mult, op1=ALU.add).then_inc(s_comb, 1)

            for n, what in enumerate(ORDER[:4]):
                low_part(0, 0, n // 2, what[0])

            def body(it, first, last):
                for t in range(2 * TPP):
                    j, st = t // TPP, t % TPP
                    g, pair = it * 2 * TPP + t, 2 * it + j
                    dve.wait_ge(s_score, g + 1)
                    nc.vector.tensor_reduce(nmax[:, t % 2, :], p_score[t % 2][:, :, :], AXX, ALU.max,
                                            negate=True).then_inc(s_max, 1)
                    dve.wait_ge(s_max, g + 1)
                    nc.vector.tensor_scalar(nbias[:, t % 2, :], nmax[:, t % 2, :], SCALE, None,
                                            ALU.mult).then_inc(s_nbias, 1)
                    if not (first and t < 1):
                        reciprocals(g - 1, (t - 1) % 4)
                    if not (first and t < 2):
                        combine(g - 2, (t - 2) % 4, first and t < 6)
                    what = AT_STEP.get(st - 1)
                    if what and what[0] in "qk" and not (last and j == 1):
                        low_part(pair + 1, 1 - j, int(what[1]), what[0])
                    if st == 0:
                        copy_v(pair, j, first)
                        if not first:
                            copy_o(pair - 2, j)
            looped(dve, ITERS, body, peel_last=True)
            g = ITERS * 2 * TPP
            reciprocals(g - 1, 3)
            combine(g - 2, 2, False)
            combine(g - 1, 3, False)
            copy_o(2 * ITERS - 2, 0)
            copy_o(2 * ITERS - 1, 1)

        @block.tensor
        def _(pe):
            def project(pair, j, what, fresh):
                n = ORDER.index(what)
                bank = p_proj[n % 2]
                if what == "q0" and not fresh:
                    pe.wait_ge(s_vT, pair)
                elif what == "k0" and not fresh:
                    pe.wait_ge(s_v, pair)
                elif what in ("q1", "k1", "v"):
                    pe.wait_ge(s_lo, 4 * pair + n - 1)
                if what == "vt":
                    pe.wait_ge(s_lo, 4 * pair + 4)
                    pe.wait_ge(s_vT, pair + 1)
                    for k in range(QT):
                        last_op = nc.tensor.transpose(bank[:, k * P:(k + 1) * P], vT[:, k * P:(k + 1) * P], ident)
                    last_op.then_inc(s_proj, 1)
                    return
                if what == "q0":
                    pe.wait_ge(s_w[j], 16 * (pair // 2 + 1))
                u = 0 if what == "v" else int(what[1])
                for k in range(KT):
                    last_op = nc.tensor.matmul(bank[:, :], weights(j, what[0], u, k),
                                               xT[:, k, bass.ds(batch_of(pair) * S, S)],
                                               start=(k == 0), stop=(k == KT - 1))
                last_op.then_inc(s_proj, 1)

            def scores(g, j, st, pair, fresh):
                u, qt = st // QT, st % QT
                if qt == 0:
                    pe.wait_ge(s_dup[j][u], 16 * DUPS * (pair // 2 + 1))
                if not fresh:
                    pe.wait_ge(s_exp, 2 * g - 2)
                for m in range(2):
                    for part in range(2):
                        last_op = nc.tensor.matmul(p_score[st % 2][:, m, :],
                                                   qs[j][u][:, m, qt * P:(qt + 1) * P], ks[j][u][:, m, part, :],
                                                   start=(part == 0), stop=(part == 1))
                last_op.then_inc(s_score, 1)

            def transposes(g, a, fresh):
                pe.wait_ge(s_comb, g + 1)
                if not fresh:
                    pe.wait_ge(s_pT, g)
                for k in range(QT):
                    last_op = nc.tensor.transpose(p_tr[:, k, :], pm[:, a, k * P:(k + 1) * P], ident)
                last_op.then_inc(s_tr, 1)

            def times_v(pair, j, key_tiles, fresh):
                if key_tiles[0] == 0:
                    pe.wait_ge(s_pT, (pair + 1) * TPP)
                    pe.wait_ge(s_v, pair + 1)
                    if not fresh:
                        pe.wait_ge(s_o, pair)
                for k in key_tiles:
                    for u in range(2):
                        last_op = nc.tensor.matmul(p_pv[u * D:(u + 1) * D, :], v[j][:, k, u * D:(u + 1) * D],
                                                   pT[j][u][:, k, :], start=(k == 0), stop=(k == QT - 1))
                if key_tiles[-1] == QT - 1:
                    last_op.then_inc(s_pv, 1)

            for what in ORDER:
                project(0, 0, what, True)

            def body(it, first, last):
                for t in range(2 * TPP):
                    j, st = t // TPP, t % TPP
                    g, pair = it * 2 * TPP + t, 2 * it + j
                    scores(g, j, st, pair, first and t < 2)
                    if not (first and t < LAG):
                        transposes(g - LAG, (t - LAG) % 4, first and t == LAG)
                    what = AT_STEP.get(st)
                    if what and not (last and j == 1):
                        project(pair + 1, 1 - j, what, False)
                    if st in PV_STEP and not (first and j == 0):
                        times_v(pair - 1, 1 - j, PV_STEP[st], first)
            looped(pe, ITERS, body, peel_last=True)
            g = ITERS * 2 * TPP
            for t in range(LAG):
                transposes(g - LAG + t, (t - LAG) % 4, False)
            times_v(2 * ITERS - 1, 1, range(QT), False)


def ffn_stage(nc, ins, xs_d, ys_d, consts, tile_expert):
    with ExitStack() as ctx:
        def sb(name, shape, dt=F32):
            return ctx.enter_context(nc.sbuf_tensor(name, shape, dt))

        def ps(name, shape):
            return ctx.enter_context(nc.psum_tensor(name, shape, F32))

        def sem(name):
            return ctx.enter_context(nc.semaphore(name))

        w1 = [sb(f"w1_{j}", [P, KT, F]) for j in range(2)]
        w2 = [sb(f"w2_{j}", [P, FT, E]) for j in range(2)]
        b1 = [sb(f"b1_{j}", [P, FT]) for j in range(2)]
        b2 = [sb(f"b2_{j}", [P, E]) for j in range(2)]
        xs = [sb(f"xs{j}", [P, FS, E]) for j in range(2)]
        xsT = [sb(f"xsT{j}", [P, KT, FFN_TILE]) for j in range(2)]
        h = [sb(f"h{j}", [P, FT, FFN_TILE]) for j in range(2)]
        y = [sb(f"y{j}", [P, FS, E]) for j in range(2)]
        p_x = [ps(f"p_x{j}", [P, KT, FFN_TILE]) for j in range(2)]
        p_h = [ps(f"p_h{j}", [P, 2, FFN_TILE]) for j in range(2)]
        p_y = [ps(f"p_y{j}", [P, FS, E]) for j in range(2)]
        s_xs, s_w1 = [sem(f"f_xs{j}") for j in range(2)], [sem(f"f_w1{j}") for j in range(2)]
        s_w2, s_st = [sem(f"f_w2{j}") for j in range(2)], [sem(f"f_st{j}") for j in range(2)]
        s_tr, s_xT, s_h, s_gelu, s_y, s_yb = sem("f_tr"), sem("f_xT"), sem("f_h"), sem("f_gelu"), sem("f_y"), sem("f_yb")
        ident = consts[:, C_ID:C_ID + P]
        xs_v = xs_d.rearrange("(n s p) e -> n p s e", s=FS, p=P)
        ys_v = ys_d.rearrange("(n s p) e -> n p s e", s=FS, p=P)
        HG = FT // 2
        LOOPED = FFN_TILES - 1
        assert LOOPED % 2 == 0

        def tiles_of(engine, body):
            body(0, 0, 0, True, True)
            body(1, 1, 0, False, True)
            body(2, 0, 1, False, False)
            with engine.Fori(1, LOOPED // 2) as i:
                body(2 * i + 1, 1, i, False, False)
                body(2 * i + 2, 0, i + 1, False, False)

        block = ctx.enter_context(nc.Block())

        @block.sync
        def _(sp):
            def body(n, j, uses, first, fresh):
                e = sp.value_load(tile_expert[0:1, bass.ds(n, 1)], min_val=0, max_val=NE - 1)
                if not fresh:
                    sp.wait_ge(s_tr, n - 1)
                sp.dma_start(xs[j][:, :, :], xs_v[bass.ds(n, 1)].rearrange("a p s e -> (a p) s e")
                             ).then_inc(s_xs[j], 16)
                if not fresh:
                    sp.wait_ge(s_gelu, (n - 1) * FT)
                sp.dma_start(w1[j][:, :, :], ins["w1"][bass.ds(e, 1)].rearrange("a p k f -> (a p) k f")
                             ).then_inc(s_w1[j], 16)
                sp.dma_start(b1[j][:, :], ins["b1"][bass.ds(e, 1)].rearrange("a p f -> (a p) f")
                             ).then_inc(s_w1[j], 16)
                if not fresh:
                    sp.wait_ge(s_yb, n - 1)
                sp.dma_start(w2[j][:, :, :], ins["w2"][bass.ds(e, 1)].rearrange("a p k f -> (a p) k f")
                             ).then_inc(s_w2[j], 16)
                sp.dma_start(b2[j][:, :], ins["b2"][bass.ds(e, 1)].rearrange("a p f -> (a p) f")
                             ).then_inc(s_w2[j], 16)
            tiles_of(sp, body)

        @block.gpsimd
        def _(pool):
            def body(n, j, uses, first, fresh):
                pool.wait_ge(s_yb, n + 1)
                pool.dma_start(ys_v[bass.ds(n, 1)].rearrange("a p s e -> (a p) s e"), y[j][:, :, :]
                               ).then_inc(s_st[j], 16)
            tiles_of(pool, body)
            pool.wait_ge(s_st[0], 16 * (LOOPED // 2 + 1))
            pool.wait_ge(s_st[1], 16 * (LOOPED // 2))

        @block.scalar
        def _(act):
            def body(n, j, uses, first, fresh):
                act.wait_ge(s_w1[j], 32 * (uses + 1))
                if not fresh:
                    act.wait_ge(s_y, n - 1)
                for f in range(FT):
                    act.wait_ge(s_h, n * HG + f // 2 + 1)
                    nc.scalar.activation(h[j][:, f, :], p_h[(f // 2) % 2][:, f % 2, :], ACT.Gelu_apprx_tanh,
                                         bias=b1[j][:, f:f + 1]).then_inc(s_gelu, 1)
            tiles_of(act, body)

        @block.vector
        def _(dve):
            def body(n, j, uses, first, fresh):
                dve.wait_ge(s_tr, n + 1)
                if not fresh:
                    dve.wait_ge(s_h, (n - 1) * HG)
                nc.vector.tensor_copy(xsT[j][:, :, :], p_x[j][:, :, :]).then_inc(s_xT, 1)
                if not first:
                    add_b2(n - 1, 1 - j, uses if j == 1 else uses - 1, fresh)

            def add_b2(n, j, uses, fresh):
                dve.wait_ge(s_y, n + 1)
                dve.wait_ge(s_w2[j], 32 * (uses + 1))
                if not fresh:
                    dve.wait_ge(s_st[j], 16 * uses)
                nc.vector.tensor_tensor(y[j][:, :, :], p_y[j][:, :, :],
                                        b2[j][:, :].unsqueeze(1).to_broadcast([P, FS, E]), ALU.add
                                        ).then_inc(s_yb, 1)
            body(0, 0, 0, True, True)
            body(1, 1, 0, False, True)
            dve.wait_ge(s_tr, 3)
            dve.wait_ge(s_h, HG)
            nc.vector.tensor_copy(xsT[0][:, :, :], p_x[0][:, :, :]).then_inc(s_xT, 1)
            add_b2(1, 1, 0, True)
            with dve.Fori(1, LOOPED // 2) as i:
                body(2 * i + 1, 1, i, False, False)
                body(2 * i + 2, 0, i + 1, False, False)
            add_b2(FFN_TILES - 1, 0, LOOPED // 2, False)

        @block.tensor
        def _(pe):
            def transposes(n, j, uses, fresh):
                pe.wait_ge(s_xs[j], 16 * (uses + 1))
                if not fresh:
                    pe.wait_ge(s_xT, n - 1)
                for k in range(KT):
                    for s in range(FS):
                        last_op = nc.tensor.transpose(p_x[j][:, k, s * P:(s + 1) * P],
                                                      xs[j][:, s, k * P:(k + 1) * P], ident)
                last_op.then_inc(s_tr, 1)

            def body(n, j, uses, first, fresh, last=False):
                pe.wait_ge(s_xT, n + 1)
                pe.wait_ge(s_w1[j], 32 * (uses + 1))
                for g in range(HG):
                    if not (first and g < 2):
                        pe.wait_ge(s_gelu, (n * HG + g - 1) * 2)
                    for f in range(2 * g, 2 * g + 2):
                        for k in range(KT):
                            last_op = nc.tensor.matmul(p_h[g % 2][:, f % 2, :], w1[j][:, k, f * P:(f + 1) * P],
                                                       xsT[j][:, k, :], start=(k == 0), stop=(k == KT - 1))
                    last_op.then_inc(s_h, 1)
                if not last:
                    transposes(n + 1, 1 - j, (uses if j == 0 else uses + 1), first)
                pe.wait_ge(s_w2[j], 32 * (uses + 1))
                pe.wait_ge(s_gelu, (n + 1) * FT)
                if not fresh:
                    pe.wait_ge(s_yb, n - 1)
                for s in range(FS):
                    for f in range(FT):
                        last_op = nc.tensor.matmul(p_y[j][:, s, :], h[j][:, f, s * P:(s + 1) * P], w2[j][:, f, :],
                                                   start=(f == 0), stop=(f == FT - 1))
                last_op.then_inc(s_y, 1)

            transposes(0, 0, 0, True)
            body(0, 0, 0, True, True)
            body(1, 1, 0, False, True)
            body(2, 0, 1, False, False)
            with pe.Fori(1, LOOPED // 2 - 1) as i:
                body(2 * i + 1, 1, i, False, False)
                body(2 * i + 2, 0, i + 1, False, False)
            i = LOOPED // 2 - 1
            body(2 * i + 1, 1, i, False, False)
            body(2 * i + 2, 0, i + 1, False, False, last=True)


def output_stage(nc, ins, oT_d, ys_d, slot_u, prob, out):
    G = 2 * P
    with ExitStack() as ctx:
        def sb(name, shape, dt=F32):
            return ctx.enter_context(nc.sbuf_tensor(name, shape, dt))

        def sem(name):
            return ctx.enter_context(nc.semaphore(name))

        wo = sb("wo", [P, PAIRS, E])
        rows = sb("rows", [P, 3, E])
        oTs = [sb(f"oTs{j}", [P, PAIRS, G]) for j in range(2)]
        x = [sb(f"x{j}", [P, 2, E]) for j in range(2)]
        ff = [[sb(f"ff{j}{s}", [P, E]) for s in range(2)] for j in range(2)]
        yb, yn = [sb(f"yb{j}", [P, 2, E]) for j in range(2)], [sb(f"yn{j}", [P, 2, E]) for j in range(2)]
        acc = [sb(f"acc{j}", [P, 2, E]) for j in range(2)]
        stats, mom = sb("ostats", [P, 2, 6]), sb("omom", [P, 6, 2])
        s_root = sem("o_root")
        p_y = [ctx.enter_context(nc.psum_tensor(f"po{j}", [P, 2, E], F32)) for j in range(2)]
        s_c, s_sc = sem("o_c"), sem("o_sc")
        s_o, s_x = [sem(f"o_o{j}") for j in range(2)], [sem(f"o_x{j}") for j in range(2)]
        s_ff, s_st = [sem(f"o_ff{j}") for j in range(2)], [sem(f"o_st{j}") for j in range(2)]
        s_y, s_d, s_res, s_out = sem("o_y"), sem("o_d"), sem("o_res"), sem("o_out")
        steps = T // G // 2
        DVE_STEPS = MOMENT_STEPS + 5
        x_v = ins["x"].rearrange("(n s p) e -> n p s e", s=2, p=P)
        out_v = out.rearrange("(n s p) e -> n p s e", s=2, p=P)
        oT_v = oT_d.rearrange("h p t -> p h t")
        bro = [P, 2, E]

        def row(i):
            return rows[:, i, :].unsqueeze(1).to_broadcast(bro)

        block = ctx.enter_context(nc.Block())

        @block.sync
        def _(sp):
            sp.dma_start(wo[:, :, :], ins["wo"]).then_inc(s_c, 16)
            sp.dma_start(rows[:, :, :], ins["out_rows"]).then_inc(s_c, 16)

            def load(n, j, fresh):
                if not fresh:
                    sp.wait_ge(s_y, n - 1)
                sp.dma_start(oTs[j][:, :, :], oT_v[:, :, bass.ds(n * G, G)]).then_inc(s_o[j], 16)
                if not fresh:
                    sp.wait_ge(s_res, n - 1)
                sp.dma_start(x[j][:, :, :], x_v[bass.ds(n, 1)].rearrange("a p s e -> (a p) s e")
                             ).then_inc(s_x[j], 16)

            def store(n, j):
                sp.wait_ge(s_out, 2 * n + 2)
                sp.dma_start(out_v[bass.ds(n, 1)].rearrange("a p s e -> (a p) s e"), acc[j][:, :, :]
                             ).then_inc(s_st[j], 16)

            load(0, 0, True)
            load(1, 1, True)

            def body(i, first, last):
                for j in range(2):
                    n = 2 * i + j
                    store(n, j)
                    if not last:
                        load(n + 2, j, False)
            looped(sp, steps, body, peel_last=True)
            for j in range(2):
                sp.wait_ge(s_st[j], 16 * steps)

        @block.gpsimd
        def _(pool):
            for n in range(2 * steps):
                j = n % 2
                if n >= 2:
                    pool.wait_ge(s_out, 2 * n - 2)
                for s in range(2):
                    c = 2 * n + s
                    pool.indirect_dma_start(
                        out=ff[j][s][:, :], out_offset=None, in_=ys_d,
                        in_offset=bass.IndirectOffsetOnAxis(ap=slot_u[:, c:c + 1], axis=0)
                    ).then_inc(s_ff[j], 16)

        @block.scalar
        def _(act):
            def body(i, first, last):
                for j in range(2):
                    act.wait_ge(s_d, DVE_STEPS * (2 * i + j) + 2 + RECIPROCAL_STEP)
                    nc.scalar.activation(mom[:, 5, :], mom[:, 4, :], ACT.Sqrt).then_inc(s_root, 1)
            looped(act, steps, body)

        @block.tensor
        def _(pe):
            pe.wait_ge(s_c, 32)

            def body(i, first, last):
                for j in range(2):
                    n = 2 * i + j
                    pe.wait_ge(s_o[j], 16 * (i + 1))
                    if not first:
                        pe.wait_ge(s_d, DVE_STEPS * (n - 2) + 1)
                    for s in range(2):
                        for k in range(PAIRS):
                            last_op = nc.tensor.matmul(p_y[j][:, s, :], oTs[j][:, k, s * P:(s + 1) * P], wo[:, k, :],
                                                       start=(k == 0), stop=(k == PAIRS - 1))
                    last_op.then_inc(s_y, 1)
            looped(pe, steps, body)

        @block.vector
        def _(dve):
            v = nc.vector
            dve.wait_ge(s_c, 32)
            v.tensor_scalar(rows[:, 1:3, :], rows[:, 1:3, :], OUT_SCALE, None, ALU.mult).then_inc(s_sc, 1)
            dve.wait_ge(s_sc, 1)

            def body(i, first, last):
                for j in range(2):
                    n = 2 * i + j
                    done = [0]

                    def step(ins_):
                        done[0] += 1
                        ins_.then_inc(s_d, 1)
                        dve.wait_ge(s_d, DVE_STEPS * n + done[0])

                    dve.wait_ge(s_y, n + 1)
                    step(v.tensor_tensor(yb[j][:, :, :], p_y[j][:, :, :], row(0), ALU.add))
                    for s in range(2):
                        last_op = v.bn_stats(stats[:, s, :], yb[j][:, s, :])
                    step(last_op)
                    moments(nc, dve, step, stats, mom, s_root, n + 1)
                    for s in range(2):
                        last_op = v.tensor_scalar(yn[j][:, s, :], yb[j][:, s, :], mom[:, 0, s:s + 1], mom[:, 1, s:s + 1],
                                                  ALU.subtract, ALU.mult)
                    step(last_op)
                    step(v.tensor_tensor(yn[j][:, :, :], yn[j][:, :, :], row(1), ALU.mult))
                    step(v.tensor_tensor(yn[j][:, :, :], yn[j][:, :, :], row(2), ALU.add))
                    dve.wait_ge(s_x[j], 16 * (i + 1))
                    v.tensor_tensor(yn[j][:, :, :], yn[j][:, :, :], x[j][:, :, :], ALU.add).then_inc(s_res, 1)
                    dve.wait_ge(s_res, n + 1)
                    dve.wait_ge(s_ff[j], 32 * (i + 1))
                    if not first:
                        dve.wait_ge(s_st[j], 16 * i)
                    for s in range(2):
                        v.scalar_tensor_tensor(out=acc[j][:, s, :], in0=ff[j][s][:, :],
                                               scalar=prob[:, bass.ds(2 * n + s, 1)], in1=yn[j][:, s, :],
                                               op0=ALU.mult, op1=ALU.add).then_inc(s_out, 1)
            looped(dve, steps, body)


def build(nc, ins, out):
    xn_d = nc.dram_tensor("xn_scratch", [T, E], F32).ap()
    xs_d = nc.dram_tensor("xs_scratch", [SLOTS, E], F32).ap()
    ys_d = nc.dram_tensor("ys_scratch", [SLOTS, E], F32).ap()
    oT_d = nc.dram_tensor("oT_scratch", [PAIRS, P, T], F32).ap()
    with ExitStack() as ctx:
        def sb(name, shape, dt=F32):
            return ctx.enter_context(nc.sbuf_tensor(name, shape, dt))

        consts = sb("consts", [P, CONSTS])
        slot_u, prob = sb("slot_u", [P, NT], U32), sb("prob", [P, NT])
        tile_expert = sb("tile_expert", [P, FFN_TILES], I32)
        with ExitStack() as att:
            xT = att.enter_context(nc.sbuf_tensor("xT", [P, KT, T], F32))
            with ExitStack() as routing:
                sw = routing.enter_context(nc.sbuf_tensor("sw", [P, KT, NE], F32))
                pL = routing.enter_context(nc.psum_tensor("pL", [P, 512], F32))
                norm_stage(nc, ins, xn_d, xs_d, xT, consts, sw, pL)
                route_stage(nc, ins, consts, pL, slot_u, prob, tile_expert)
            attention_stage(nc, ins, xn_d, xs_d, oT_d, xT, consts, slot_u)
        ffn_stage(nc, ins, xs_d, ys_d, consts, tile_expert)
        output_stage(nc, ins, oT_d, ys_d, slot_u, prob, out)


def kernel(L0_attn_X, L0_attn_Wq, L0_attn_bq, L0_attn_Wk, L0_attn_bk, L0_attn_Wv, L0_attn_bv, L0_attn_Wo,
           L0_attn_bo, L0_attn_gamma, L0_attn_beta, L0_attn_lam, L0_ffn_switch_w, L0_ffn_switch_b,
           L0_ffn_w1, L0_ffn_b1, L0_ffn_w2, L0_ffn_b2):
    import concourse.bacc as bacc
    import numpy as np
    from concourse.bass_utils import run_bass_kernel_spmd

    def a(x):
        return np.asarray(x)

    def wide(x):
        x = a(x)
        return np.broadcast_to(x[None], (P,) + x.shape)

    def by_pair(wt, width):
        return a(wt).reshape(PAIRS, 2, KT, P, width).transpose(0, 3, 2, 1, 4).reshape(PAIRS, P, KT * 2 * width)

    idx = np.arange(P)
    consts = np.concatenate([
        np.eye(P), idx[:, None] < idx[None, :],
        np.broadcast_to(np.arange(MAXT) * FFN_TILE, (P, MAXT)),
        np.broadcast_to(np.arange(FFN_TILES), (P, FFN_TILES))], axis=1).astype(np.float32)
    arrays = {
        "x": a(L0_attn_X).reshape(T, E),
        "consts": consts,
        "sw": a(L0_ffn_switch_w).reshape(KT, P, NE).transpose(1, 0, 2),
        "swb": wide(L0_ffn_switch_b),
        "w_attn": np.concatenate([by_pair(L0_attn_Wq, 2 * D), by_pair(L0_attn_Wk, 2 * D),
                                  by_pair(L0_attn_Wv, D)], axis=2),
        "attn_bias": np.concatenate([a(L0_attn_bq).T, a(L0_attn_bk).T,
                                     a(L0_attn_bv).reshape(PAIRS, P).T], axis=1),
        "lam": np.broadcast_to(a(L0_attn_lam).reshape(1, 1), (P, 1)),
        "w1": a(L0_ffn_w1).reshape(NE, KT, P, F).transpose(0, 2, 1, 3),
        "w2": a(L0_ffn_w2).reshape(NE, FT, P, E).transpose(0, 2, 1, 3),
        "b1": a(L0_ffn_b1).reshape(NE, FT, P).transpose(0, 2, 1),
        "b2": np.broadcast_to(a(L0_ffn_b2)[:, None, :], (NE, P, E)),
        "wo": a(L0_attn_Wo).reshape(PAIRS, P, E).transpose(1, 0, 2),
        "out_rows": np.stack([wide(L0_attn_bo), wide(L0_attn_gamma), wide(L0_attn_beta)], axis=1),
    }
    arrays = {k: np.ascontiguousarray(x) for k, x in arrays.items()}
    nc = bacc.Bacc("TRN2", target_bir_lowering=False, num_devices=1)
    ins = {k: nc.dram_tensor("in_" + k, x.shape, F32, kind="ExternalInput").ap() for k, x in arrays.items()}
    out = nc.dram_tensor("out", [T, E], F32, kind="ExternalOutput").ap()
    build(nc, ins, out)
    r = run_bass_kernel_spmd(nc, [{"in_" + k: x for k, x in arrays.items()}], core_ids=[0])
    return r.results[0]["out"].reshape(B, S, E)
```

```python
from contextlib import ExitStack

import concourse.bass as bass
from concourse import mybir

F32 = mybir.dt.float32
F32R = mybir.dt.float32r
I32 = mybir.dt.int32
U32 = mybir.dt.uint32
ALU = mybir.AluOpType
ACT = mybir.ActivationFunctionType
AXX = mybir.AxisListType.X

P = 128
B, S, E = 8, 512, 256
H, D = 16, 64
T = B * S
NT = T // P
KT = E // P
EPS = 1e-5
SCALE = float(D) ** -0.5
OUT_SCALE = 1.0 - 0.8
NE, F = 8, 1024
FT = F // P
FFN_TILE = 256
FFN_TILES = (T + NE * (FFN_TILE - 1)) // FFN_TILE
SLOTS = FFN_TILES * FFN_TILE
FS = FFN_TILE // P
MAXT = T // FFN_TILE
PAIRS = H // 2
QT = S // P
TPP = 2 * QT
ITERS = B * PAIRS // 2
WPAIR = KT * (2 * P + 2 * P + 2 * D)
C_ID, C_UP, C_J, C_T = 0, P, 2 * P, 2 * P + MAXT
C_TOKEN = C_T + FFN_TILES
CONSTS = C_TOKEN + NT


def looped(engine, count, body, peel_last=False):
    body(0, True, False)
    end = count - 1 if peel_last else count
    with engine.Fori(1, end) as turn:
        body(turn, False, False)
    if peel_last:
        body(count - 1, False, True)


MOMENT_STEPS, RECIPROCAL_STEP = 9, 5


def moments(nc, dve, step, stats, mom, s_root, roots):
    v = nc.vector
    mean, rstd, dif, ve, rec, root = (mom[:, k, :] for k in range(6))
    v.tensor_tensor(mean, stats[:, :, 1], stats[:, :, 4], ALU.add)
    v.tensor_tensor(dif, stats[:, :, 1], stats[:, :, 4], ALU.subtract)
    step(v.tensor_tensor(ve, stats[:, :, 2], stats[:, :, 5], ALU.add))
    v.tensor_scalar(mean, mean, 0.5, None, ALU.mult)
    v.tensor_scalar(dif, dif, 0.5, None, ALU.mult)
    step(v.tensor_scalar(ve, ve, 1.0 / E, EPS, ALU.mult, ALU.add))
    step(v.tensor_tensor(dif, dif, dif, ALU.mult))
    step(v.tensor_tensor(ve, ve, dif, ALU.add))
    step(v.reciprocal(rec, ve))
    dve.wait_ge(s_root, roots)
    step(v.tensor_tensor(dif, root, root, ALU.mult))
    step(v.tensor_tensor(dif, dif, ve, ALU.mult))
    step(v.tensor_scalar(dif, dif, -0.5, 1.5, ALU.mult, ALU.add))
    step(v.tensor_tensor(rstd, root, dif, ALU.mult))


class WeightParts:

    def __init__(self, nc, ctx, ins, wp_d, name, first_pair, count):
        def sem(what):
            return ctx.enter_context(nc.semaphore(f"{name}_{what}"))

        self.nc, self.w_d, self.wp_d, self.first_pair, self.count = nc, ins["w_attn"], wp_d, first_pair, count
        self.w = ctx.enter_context(nc.sbuf_tensor(f"{name}_w", [P, WPAIR], F32))
        self.parts = ctx.enter_context(nc.sbuf_tensor(f"{name}_parts", [P, 2, WPAIR], F32R))
        self.s_w, self.s_scaled, self.s_high, self.s_low, self.s_stored = (
            sem(what) for what in ("w", "scaled", "high", "low", "stored"))

    def load(self, sp, k):
        src = self.w_d[bass.ds(self.first_pair + k, 1)].rearrange("c p n -> (c p) n")
        sp.dma_start(self.w[:, :], src).then_inc(self.s_w, 16)

    def sync(self, sp, k, last):
        sp.wait_ge(self.s_low, k + 1)
        if not last:
            self.load(sp, k + 1)
        dst = self.wp_d[bass.ds(self.first_pair + k, 1)].rearrange("c p a n -> (c p) a n")
        sp.dma_start(dst, self.parts[:, :, :].bitcast(F32)).then_inc(self.s_stored, 16)

    def scalar(self, act, k, first):
        act.wait_ge(self.s_w, 16 * (k + 1))
        wq = self.w[:, 0:KT * 2 * P]
        self.nc.scalar.activation(wq, wq, ACT.Identity, scale=SCALE).then_inc(self.s_scaled, 1)
        act.wait_ge(self.s_scaled, k + 1)
        if not first:
            act.wait_ge(self.s_stored, 16 * k)
        self.nc.scalar.copy(self.parts[:, 0, :], self.w[:, :]).then_inc(self.s_high, 1)

    def gpsimd(self, pool, k):
        pool.wait_ge(self.s_high, k + 1)
        self.nc.gpsimd.tensor_tensor(self.parts[:, 1, :], self.w[:, :], self.parts[:, 0, :].bitcast(F32),
                                     ALU.subtract).then_inc(self.s_low, 1)

    def finish(self, sp):
        sp.wait_ge(self.s_stored, 16 * self.count)


def norm_stage(nc, ins, wp_d, xn_d, xT, consts, sw, pL):
    G = 2 * P
    TURN = 4
    TURNS = T // G // TURN
    with ExitStack() as ctx:
        def sb(name, shape, dt=F32):
            return ctx.enter_context(nc.sbuf_tensor(name, shape, dt))

        def sem(name):
            return ctx.enter_context(nc.semaphore(name))

        xin = [sb(f"xin{j}", [P, 2, E]) for j in range(TURN)]
        xn = [sb(f"xn{j}", [P, 2, E]) for j in range(TURN)]
        xt = [sb(f"xt{a}", [P, KT, G]) for a in range(2)]
        stats, mom = sb("stats", [P, 2 * TURN, 6]), sb("mom", [P, 6, 2 * TURN])
        wparts = WeightParts(nc, ctx, ins, wp_d, "n_wt", 0, TURNS)
        pX = [ctx.enter_context(nc.psum_tensor(f"pX{a}", [P, KT, G], F32)) for a in range(2)]
        s_const = sem("n_const")
        s_x = [sem(f"n_x{j}") for j in range(TURN)]
        s_store = [sem(f"n_store{j}") for j in range(TURN)]
        s_stat, s_d, s_root, s_xn = sem("n_stat"), sem("n_dve"), sem("n_root"), sem("n_xn")
        s_tr, s_xt, s_logit = sem("n_tr"), sem("n_xt"), sem("n_logit")
        x_d = ins["x"].rearrange("(n s p) e -> n p s e", s=2, p=P)
        xn_v = xn_d.rearrange("(n s p) e -> n p s e", s=2, p=P)

        def at(ap, n):
            return ap[bass.ds(n, 1)].rearrange("a p s e -> (a p) s e")

        block = ctx.enter_context(nc.Block())

        @block.sync
        def _(sp):
            for j in range(TURN):
                sp.dma_start(xin[j][:, :, :], at(x_d, j)).then_inc(s_x[j], 16)
            sp.dma_start(consts[:, :], ins["consts"]).then_inc(s_const, 16)
            sp.dma_start(sw[:, :, :], ins["sw"]).then_inc(s_const, 16)
            wparts.load(sp, 0)

            def body(i, first, last):
                for j in range(TURN):
                    n = TURN * i + j
                    sp.wait_ge(s_xn, n + 1)
                    if not last:
                        sp.dma_start(xin[j][:, :, :], at(x_d, n + TURN)).then_inc(s_x[j], 16)
                    sp.dma_start(at(xn_v, n), xn[j][:, :, :]).then_inc(s_store[j], 16)
                wparts.sync(sp, i, last)
            looped(sp, TURNS, body, peel_last=True)
            for j in range(TURN):
                sp.wait_ge(s_store[j], 16 * TURNS)
            wparts.finish(sp)

        @block.gpsimd
        def _(pool):
            looped(pool, TURNS, lambda i, first, last: wparts.gpsimd(pool, i))

        @block.vector
        def _(dve):
            def body(i, first, last):
                done = [0]

                def step(ins_):
                    done[0] += 1
                    ins_.then_inc(s_d, 1)
                    dve.wait_ge(s_d, MOMENT_STEPS * i + done[0])

                for j in range(TURN):
                    dve.wait_ge(s_x[j], 16 * (i + 1))
                    for s in range(2):
                        nc.vector.bn_stats(stats[:, 2 * j + s, :], xin[j][:, s, :]).then_inc(s_stat, 1)
                dve.wait_ge(s_stat, 2 * TURN * (i + 1))
                moments(nc, dve, step, stats, mom, s_root, i + 1)
                for j in range(TURN):
                    n = TURN * i + j
                    if not first:
                        dve.wait_ge(s_tr, n - TURN + 1)
                        dve.wait_ge(s_store[j], 16 * i)
                    for s in range(2):
                        a = 2 * j + s
                        last_op = nc.vector.tensor_scalar(xn[j][:, s, :], xin[j][:, s, :], mom[:, 0, a:a + 1],
                                                          mom[:, 1, a:a + 1], ALU.subtract, ALU.mult)
                    last_op.then_inc(s_xn, 1)
            looped(dve, TURNS, body)

        @block.scalar
        def _(act):
            def root(i):
                act.wait_ge(s_d, MOMENT_STEPS * i + RECIPROCAL_STEP)
                nc.scalar.activation(mom[:, 5, :], mom[:, 4, :], ACT.Sqrt).then_inc(s_root, 1)

            def body(i, first, last):
                for j in range(TURN):
                    n, a = TURN * i + j, j % 2
                    if j == 2:
                        wparts.scalar(act, i, first)
                    act.wait_ge(s_tr, n + 1)
                    if not (first and j < 2):
                        act.wait_ge(s_logit, n - 1)
                    nc.scalar.copy(xt[a][:, :, :], pX[a][:, :, :])
                    nc.scalar.copy(xT[:, :, bass.ds(n * G, G)], pX[a][:, :, :]).then_inc(s_xt, 1)
                    if j == 1 and not last:
                        root(i + 1)
            root(0)
            looped(act, TURNS, body, peel_last=True)

        @block.tensor
        def _(pe):
            pe.wait_ge(s_const, 32)
            ident = consts[:, C_ID:C_ID + P]

            def body(i, first, last):
                for j in range(TURN):
                    n, a = TURN * i + j, j % 2
                    pe.wait_ge(s_xn, n + 1)
                    if not (first and j < 2):
                        pe.wait_ge(s_xt, n - 1)
                    for k in range(KT):
                        for s in range(2):
                            last_op = nc.tensor.transpose(pX[a][:, k, s * P:(s + 1) * P],
                                                          xn[j][:, s, k * P:(k + 1) * P], ident)
                    last_op.then_inc(s_tr, 1)
                    if not (first and j == 0):
                        logits(n - 1, 1 - a)

            def logits(n, a):
                pe.wait_ge(s_xt, n + 1)
                for s in range(2):
                    for k in range(KT):
                        last_op = nc.tensor.matmul(pL[:, bass.ds((n * 2 + s) * NE, NE)],
                                                   xt[a][:, k, s * P:(s + 1) * P], sw[:, k, :],
                                                   start=(k == 0), stop=(k == KT - 1))
                last_op.then_inc(s_logit, 1)

            looped(pe, TURNS, body)
            logits(TURNS * TURN - 1, 1)


def route_stage(nc, ins, wp_d, token_d, xT, xp, w_first, consts, pL, slot_u, prob, tile_expert):
    with ExitStack() as ctx:
        def sb(name, shape, dt=F32):
            return ctx.enter_context(nc.sbuf_tensor(name, shape, dt))

        def sem(name):
            return ctx.enter_context(nc.semaphore(name))

        swb, weight = sb("swb", [P, NE]), sb("weight", [P, NE])
        lg, ex, oh = sb("lg", [P, NT, NE]), sb("ex", [P, NT, NE]), sb("oh", [P, NT, NE])
        col, den = sb("col", [P, NT]), sb("den", [P, NT])
        inc, exc = sb("inc", [P, NE, NT]), sb("exc", [P, NE, NT])
        ones, upper = sb("ones", [P, P]), consts[:, C_UP:C_UP + P]
        more = sb("more", [P, NE, MAXT])
        tiles, tile_end, base = sb("tiles", [P, NE]), sb("tile_end", [P, NE]), sb("base", [P, NE])
        slot_f = sb("slot_f", [P, NT])
        past, te_f = sb("past", [P, FFN_TILES, NE]), sb("te_f", [P, FFN_TILES])
        pR = ctx.enter_context(nc.psum_tensor("pR", [P, NT, NE], F32))
        pC = ctx.enter_context(nc.psum_tensor("pC", [P, NT, NE], F32))
        wparts = WeightParts(nc, ctx, ins, wp_d, "r_wt", PAIRS // 2, PAIRS // 2)
        no_token = sb("no_token", [P, SLOTS // P])
        s_zero, s_zeroed, s_xhi, s_xlo, s_wfirst = (
            sem("r_zero"), sem("r_zeroed"), sem("r_xhi"), sem("r_xlo"), sem("r_wfirst"))
        x_parts = [xp[:, 0, part, :, :] for part in range(2)]
        s_in, s_d, s_e, s_rank, s_p = sem("r_in"), sem("r_dve"), sem("r_exp"), sem("r_rank"), sem("r_pool")
        block = ctx.enter_context(nc.Block())
        SHIFTED, ONEHOT = 3, 9

        @block.sync
        def _(sp):
            sp.dma_start(swb[:, :], ins["swb"]).then_inc(s_in, 16)
            wparts.load(sp, 0)
            for j in range(2):
                sp.dma_start(w_first[j][:, :, :].bitcast(F32), wp_d[j]).then_inc(s_wfirst, 16)
            sp.wait_ge(s_zero, 1)
            sp.dma_start(token_d.rearrange("(p n) a -> p (n a)", p=P), no_token[:, :]).then_inc(s_zeroed, 16)
            for k in range(wparts.count):
                wparts.sync(sp, k, k == wparts.count - 1)
            wparts.finish(sp)
            sp.wait_ge(s_wfirst, 32)
            sp.wait_ge(s_zeroed, 16)

        @block.gpsimd
        def _(pool):
            nc.gpsimd.memset(ones[:, :], 1.0).then_inc(s_p, 1)
            for e in range(NE):
                last_op = nc.gpsimd.memset(weight[:, e:e + 1], float(NE - e))
            last_op.then_inc(s_p, 1)
            nc.gpsimd.memset(no_token[:, :], 0.0).then_inc(s_zero, 1)
            pool.wait_ge(s_xhi, 1)
            nc.gpsimd.tensor_tensor(x_parts[1], xT[:, :, 0:S], x_parts[0].bitcast(F32), ALU.subtract
                                    ).then_inc(s_xlo, 1)
            for k in range(wparts.count):
                wparts.gpsimd(pool, k)

        @block.scalar
        def _(act):
            nc.scalar.copy(x_parts[0], xT[:, :, 0:S]).then_inc(s_xhi, 1)
            act.wait_ge(s_d, SHIFTED)
            nc.scalar.activation(ex[:, :, :], lg[:, :, :], ACT.Exp).then_inc(s_e, 1)
            for k in range(wparts.count):
                wparts.scalar(act, k, k == 0)

        @block.tensor
        def _(pe):
            pe.wait_ge(s_p, 2)
            pe.wait_ge(s_d, ONEHOT)
            nc.tensor.matmul(pR[:, :, :], upper, oh[:, :, :], start=True, stop=True)
            nc.tensor.matmul(pC[:, :, :], ones[:, :], oh[:, :, :], start=True, stop=True).then_inc(s_rank, 1)

        @block.vector
        def _(dve):
            done = [0]

            def step(ins_):
                done[0] += 1
                ins_.then_inc(s_d, 1)
                dve.wait_ge(s_d, done[0])

            tne, v = [P, NT, NE], nc.vector
            pLv = pL[:, 0:NT * NE].rearrange("p (t e) -> p t e", e=NE)
            dve.wait_ge(s_in, 16)
            step(v.tensor_tensor(lg[:, :, :], pLv, swb[:, :].unsqueeze(1).to_broadcast(tne), ALU.add))
            step(v.tensor_reduce(col[:, :], lg[:, :, :], AXX, ALU.max))
            step(v.tensor_tensor(lg[:, :, :], lg[:, :, :], col[:, :].unsqueeze(2).to_broadcast(tne), ALU.subtract))
            dve.wait_ge(s_p, 2)
            dve.wait_ge(s_e, 1)
            step(v.tensor_reduce(den[:, :], ex[:, :, :], AXX, ALU.add))
            step(v.reciprocal(prob[:, :], den[:, :]))
            step(v.tensor_scalar(oh[:, :, :], lg[:, :, :], 0.0, None, ALU.is_equal))
            step(v.tensor_tensor(ex[:, :, :], oh[:, :, :], weight[:, :].unsqueeze(1).to_broadcast(tne), ALU.mult))
            step(v.tensor_reduce(col[:, :], ex[:, :, :], AXX, ALU.max))
            step(v.tensor_tensor(oh[:, :, :], ex[:, :, :], col[:, :].unsqueeze(2).to_broadcast(tne), ALU.is_equal))
            dve.wait_ge(s_rank, 1)
            cnt = pC[:, :, :].rearrange("p t e -> p e t")
            for e in range(NE):
                last_op = v.tensor_tensor_scan(inc[:, e, :], ones[:, 0:NT], cnt[:, e, :], 0.0, ALU.mult, ALU.add)
            step(last_op)
            step(v.tensor_tensor(exc[:, :, :], inc[:, :, :], cnt, ALU.subtract))
            em = [P, NE, MAXT]
            step(v.tensor_tensor(more[:, :, :], inc[:, :, NT - 1:NT].to_broadcast(em),
                                 consts[:, C_J:C_J + MAXT].unsqueeze(1).to_broadcast(em), ALU.is_gt))
            step(v.tensor_reduce(tiles[:, :], more[:, :, :], AXX, ALU.add))
            step(v.tensor_tensor_scan(tile_end[:, :], ones[:, 0:NE], tiles[:, :], 0.0, ALU.mult, ALU.add))
            step(v.tensor_tensor(base[:, :], tile_end[:, :], tiles[:, :], ALU.subtract))
            step(v.tensor_scalar(base[:, :], base[:, :], float(FFN_TILE), None, ALU.mult))
            step(v.tensor_tensor(lg[:, :, :], pR[:, :, :], exc[:, :, :].rearrange("p e t -> p t e"), ALU.add))
            step(v.tensor_tensor(lg[:, :, :], lg[:, :, :], base[:, :].unsqueeze(1).to_broadcast(tne), ALU.add))
            step(v.tensor_tensor(lg[:, :, :], lg[:, :, :], oh[:, :, :], ALU.mult))
            step(v.tensor_reduce(slot_f[:, :], lg[:, :, :], AXX, ALU.add))
            step(v.tensor_copy(slot_u[:, :], slot_f[:, :]))
            fe = [P, FFN_TILES, NE]
            step(v.tensor_tensor(past[:, :, :], tile_end[:, :].unsqueeze(1).to_broadcast(fe),
                                 consts[:, C_T:C_T + FFN_TILES].unsqueeze(2).to_broadcast(fe), ALU.is_le))
            step(v.tensor_reduce(te_f[:, :], past[:, :, :], AXX, ALU.add))
            step(v.tensor_scalar(te_f[:, :], te_f[:, :], float(NE - 1), None, ALU.min))
            step(v.tensor_copy(tile_expert[:, :], te_f[:, :]))


def attention_stage(nc, ins, wp_d, token_d, oT_d, xT, xp, w, consts, slot_u):
    with ExitStack() as ctx:
        def sb(name, shape, dt=F32):
            return ctx.enter_context(nc.sbuf_tensor(name, shape, dt))

        def ps(name, shape):
            return ctx.enter_context(nc.psum_tensor(name, shape, F32))

        def sem(name):
            return ctx.enter_context(nc.semaphore(name))

        bias = sb("bias", [P, PAIRS, 5])
        bias_of = {"q": 0, "k": 2, "v": 4}
        bias_now = [sb(f"bias_now{j}", [P, 5]) for j in range(2)]
        lam = sb("lam", [P, 1])
        parts = {"q": [sb(f"q_parts{u}", [P, 2, S], F32R) for u in range(2)],
                 "k": [sb(f"k_parts{u}", [P, 2, S], F32R) for u in range(2)]}
        qs = [[sb(f"qs{j}{u}", [P, 2, S], F32R) for u in range(2)] for j in range(2)]
        ks = [[sb(f"ks{j}{u}", [P, 2, 2, S], F32R) for u in range(2)] for j in range(2)]
        vT = sb("vT", [P, S])
        v = [sb(f"v{j}", [P, QT, P]) for j in range(2)]
        ex = sb("e", [P, 4, 2, S])
        pm = sb("pm", [P, 4, S])
        pT = [[sb(f"pT{j}{u}", [P, QT, S]) for u in range(2)] for j in range(2)]
        oT = [sb(f"oT{j}", [P, S]) for j in range(2)]
        nmax = sb("nmax", [P, 2, 2])
        rsum, rrec, coef = sb("rsum", [P, 4, 2]), sb("rrec", [P, 4, 2]), sb("coef", [P, 4, 1])
        token, token_slot = sb("token", [P, 1]), sb("token_slot", [P, 1], U32)
        p_score = [ps(f"p_score{a}", [P, 2, S]) for a in range(2)]
        p_tr, p_pv = ps("p_tr", [P, QT, P]), ps("p_pv", [P, S])
        p_proj = [ps(f"p_proj{a}", [P, S]) for a in range(2)]

        s_const, s_w, s_dup = sem("a_const"), [sem(f"a_w{j}") for j in range(2)], \
            [[sem(f"a_dup{j}{u}") for u in range(2)] for j in range(2)]
        s_xhi, s_xp, s_bias = sem("a_xhi"), sem("a_xp"), sem("a_bias")
        s_proj, s_hi, s_lo, s_vT, s_v = sem("a_proj"), sem("a_hi"), sem("a_lo"), sem("a_vT"), sem("a_v")
        s_score, s_max, s_exp = sem("a_score"), sem("a_max"), sem("a_exp")
        s_rec, s_coef, s_e1, s_comb = sem("a_rec"), sem("a_coef"), sem("a_e1"), sem("a_comb")
        s_tr, s_pT, s_pv, s_o = sem("a_tr"), sem("a_pT"), sem("a_pv"), sem("a_o")
        s_ost = [sem(f"a_ost{j}") for j in range(2)]
        s_idx, s_scat, s_lam, s_bq = sem("a_idx"), sem("a_scat"), sem("a_lam"), sem("a_bq")

        ident = consts[:, C_ID:C_ID + P]
        LAG = 4
        DUPS = 8

        ORDER = ("q0", "k0", "q1", "k1", "v", "vt")
        AT_STEP = {0: "q0", 1: "k0", 2: "q1", 3: "k1", 4: "v", 6: "vt"}
        PV_STEP = {5: (0,), 6: (1,), 7: (2, 3)}

        def batch_of(pair):
            return pair // PAIRS

        def weights(j, part, what, u, k):
            if what == "v":
                return w[j][:, part, KT * 4 * P + k * P:KT * 4 * P + (k + 1) * P]
            o = (0 if what == "q" else KT * 2 * P) + k * 2 * P + u * P
            return w[j][:, part, o:o + P]

        block = ctx.enter_context(nc.Block())

        @block.sync
        def _(sp):
            sp.dma_start(bias[:, :, :], ins["attn_bias"]).then_inc(s_const, 16)
            sp.dma_start(lam[:, :], ins["lam"]).then_inc(s_const, 16)
            for j in range(2):
                sp.nop().then_inc(s_ost[j], 16)
                sp.nop().then_inc(s_w[j], 16)

            def load_w(pair, j):
                src = wp_d[bass.ds(pair % PAIRS, 1)].rearrange("a p c n -> (a p) c n")
                sp.dma_start(w[j][:, :, :].bitcast(F32), src).then_inc(s_w[j], 16)

            def spread(j, u, what, pair):
                n = 4 * pair + 2 * u + (what == "k")
                sp.wait_ge(s_lo, n + 1)
                src = parts[what][u]
                for m in range(2):
                    a = src[m * D:(m + 1) * D]
                    if what == "q":
                        for part in range(2):
                            sp.dma_start(qs[j][u][part * D:(part + 1) * D, m, :].bitcast(F32),
                                         a[:, part, :].bitcast(F32)).then_inc(s_dup[j][u], 16)
                    else:
                        for half in range(2):
                            sp.dma_start(ks[j][u][half * D:(half + 1) * D, m, :, :].bitcast(F32),
                                         a[:, :, :].bitcast(F32)).then_inc(s_dup[j][u], 16)

            for u in range(2):
                for what in "qk":
                    spread(0, u, what, 0)

            def body(it, first, last):
                for j in range(2):
                    pair = 2 * it + j
                    nj = 1 - j
                    if not last:
                        sp.wait_ge(s_proj, 6 * pair + 5)
                        load_w(pair + 2, j)
                    if not (last and j == 1):
                        for u in range(2):
                            for what in "qk":
                                spread(nj, u, what, pair + 1)
                    if not first:
                        store_o(pair - 2, j)

            def store_o(pair, j):
                sp.wait_ge(s_o, pair + 1)
                dst = oT_d[bass.ds(pair % PAIRS, 1), :, bass.ds(batch_of(pair) * S, S)]
                sp.dma_start(dst.rearrange("a p n -> (a p) n"), oT[j][:, :]).then_inc(s_ost[j], 16)

            looped(sp, ITERS, body, peel_last=True)
            store_o(2 * ITERS - 2, 0)
            store_o(2 * ITERS - 1, 1)
            for j in range(2):
                sp.wait_ge(s_ost[j], 16 * (ITERS + 1))

        @block.gpsimd
        def _(pool):
            def pair_bias(pair, j):
                nc.gpsimd.tensor_copy(bias_now[j][:, :], bias[:, bass.ds(pair % PAIRS, 1), :]
                                      .rearrange("p a c -> p (a c)")).then_inc(s_bias, 1)

            pool.wait_ge(s_bq, 1)
            pair_bias(0, 0)
            pair_bias(1, 1)
            pool.nop().then_inc(s_xp, QT)

            def split_x(quarter):
                cols = bass.ds(quarter % (T // P) * P, P)
                place = (quarter // QT) % 2, quarter % QT
                hi, lo = (xp[:, bass.ds(place[0], 1), part, :, bass.ds(place[1] * P, P)]
                          .rearrange("p a k s -> p (a k) s") for part in range(2))
                nc.gpsimd.tensor_copy(hi, xT[:, :, cols]).then_inc(s_xhi, 1)
                pool.wait_ge(s_xhi, quarter - QT + 1)
                nc.gpsimd.tensor_tensor(lo, xT[:, :, cols], hi.bitcast(F32), ALU.subtract).then_inc(s_xp, 1)

            def body(it, first, last):
                if not first:
                    pool.wait_ge(s_scat, 16 * it)
                nc.gpsimd.tensor_copy(token_slot[:, :], slot_u[:, bass.ds(it, 1)])
                nc.gpsimd.tensor_copy(token[:, :], consts[:, bass.ds(C_TOKEN + it, 1)]).then_inc(s_idx, 1)
                for t in range(2 * TPP):
                    g = it * 2 * TPP + t
                    if t == 2:
                        pool.wait_ge(s_idx, it + 1)
                    pool.wait_ge(s_rec, g + 1)
                    e1 = ex[:, t % 4, 0, :]
                    nc.gpsimd.tensor_tensor(e1, e1, rrec[:, t % 4, 0:1].to_broadcast([P, S]), ALU.mult
                                            ).then_inc(s_e1, 1)
                    if t == 0:
                        pool.wait_ge(s_proj, 6 * 2 * it + 6)
                        split_x(it + QT)
                    if t % TPP == 5 and not last:
                        pair = 2 * it + t // TPP
                        pool.wait_ge(s_lo, 4 * pair + 4)
                        pool.wait_ge(s_vT, pair + 1)
                        pair_bias(pair + 2, t // TPP)
                    if t == 2:
                        pool.indirect_dma_start(
                            out=token_d, out_offset=bass.IndirectOffsetOnAxis(ap=token_slot[:, 0:1], axis=0),
                            in_=token[:, :], in_offset=None).then_inc(s_scat, 16)
            looped(pool, ITERS, body, peel_last=True)
            pool.wait_ge(s_scat, 16 * ITERS)

        @block.scalar
        def _(act):
            def high_part(pair, j, u, what, fresh=False):
                n = 4 * pair + 2 * u + (what == "k")
                act.wait_ge(s_proj, 6 * pair + ORDER.index(f"{what}{u}") + 1)
                if not fresh:
                    act.wait_ge(s_dup[1 - j][u], 16 * DUPS * ((pair - 1) // 2 + 1))
                if (what, u) == ("q", 0):
                    act.wait_ge(s_bias, pair + 1)
                b = bias_now[j][:, bias_of[what] + u:bias_of[what] + u + 1]
                nc.scalar.activation(parts[what][u][:, 0, :], p_proj[n % 2][:, :],
                                     ACT.Identity, bias=b).then_inc(s_hi, 1)

            def v_bias(pair, j):
                act.wait_ge(s_proj, 6 * pair + 5)
                b = bias_now[j][:, bias_of["v"]:bias_of["v"] + 1]
                nc.scalar.activation(vT[:, :], p_proj[0][:, :], ACT.Identity, bias=b).then_inc(s_vT, 1)

            def copy_pT(g, j, u, qt, pair, fresh):
                act.wait_ge(s_tr, g + 1)
                if u == qt == 0 and not fresh:
                    act.wait_ge(s_pv, pair - 1)
                nc.scalar.copy(pT[j][u][:, :, qt * P:(qt + 1) * P], p_tr[:, :, :]).then_inc(s_pT, 1)

            def copy_o(pair, j):
                act.wait_ge(s_pv, pair + 1)
                act.wait_ge(s_ost[j], 16 * (pair // 2 + 1))
                nc.scalar.copy(oT[j][:, :], p_pv[:, :]).then_inc(s_o, 1)

            for n, what in enumerate(ORDER[:4]):
                high_part(0, 0, n // 2, what[0], True)
            v_bias(0, 0)

            def body(it, first, last):
                for t in range(2 * TPP):
                    j, st = t // TPP, t % TPP
                    g, pair = it * 2 * TPP + t, 2 * it + j
                    if st == 0 and not first:
                        copy_o(pair - 2, j)
                    what = AT_STEP.get(st - 1)
                    if what and not (last and j == 1):
                        if what[0] in "qk":
                            high_part(pair + 1, 1 - j, int(what[1]), what[0])
                        elif what == "v":
                            v_bias(pair + 1, 1 - j)
                    if not (first and t < LAG):
                        lt = (t - LAG) % (2 * TPP)
                        lj, lst = lt // TPP, lt % TPP
                        lpair = pair if t % TPP >= LAG else pair - 1
                        copy_pT(g - LAG, lj, lst // QT, lst % QT, lpair, first)
                    for m in range(2):
                        act.wait_ge(s_max, g + 1)
                        if m == 0 and not (first and t < 4):
                            act.wait_ge(s_comb, g - 3)
                        nc.scalar.activation(ex[:, t % 4, m, :], p_score[t % 2][:, m, :], ACT.Exp,
                                             bias=nmax[:, t % 2, m:m + 1],
                                             accum_out=rsum[:, t % 4, m:m + 1]).then_inc(s_exp, 1)
            looped(act, ITERS, body, peel_last=True)
            g = ITERS * 2 * TPP
            for t in range(LAG):
                lst = TPP - LAG + t
                copy_pT(g - LAG + t, 1, lst // QT, lst % QT, 2 * ITERS - 1, False)
            copy_o(2 * ITERS - 2, 0)
            copy_o(2 * ITERS - 1, 1)

        @block.vector
        def _(dve):
            dve.wait_ge(s_const, 32)
            nc.vector.tensor_scalar(bias[:, :, 0:2], bias[:, :, 0:2], SCALE, None, ALU.mult).then_inc(s_bq, 1)
            nc.vector.tensor_scalar(lam[:, :], lam[:, :], -1.0, None, ALU.mult).then_inc(s_lam, 1)
            dve.wait_ge(s_bq, 1)
            dve.wait_ge(s_lam, 1)

            def low_part(pair, j, u, what):
                n = 4 * pair + 2 * u + (what == "k")
                dve.wait_ge(s_hi, n + 1)
                if (what, u) == ("q", 0):
                    dve.wait_ge(s_bias, pair + 1)
                b = bias_now[j][:, bias_of[what] + u:bias_of[what] + u + 1]
                nc.vector.scalar_tensor_tensor(out=parts[what][u][:, 1, :], in0=p_proj[n % 2][:, :], scalar=b,
                                               in1=parts[what][u][:, 0, :].bitcast(F32),
                                               op0=ALU.add, op1=ALU.subtract).then_inc(s_lo, 1)

            def copy_v(pair, j, fresh):
                dve.wait_ge(s_proj, 6 * pair + 6)
                if not fresh:
                    dve.wait_ge(s_pv, pair - 1)
                nc.vector.tensor_copy(v[j][:, :, :], p_proj[1][:, :].rearrange("p (k d) -> p k d", d=P)
                                      ).then_inc(s_v, 1)

            def reciprocals(g, b):
                dve.wait_ge(s_exp, 2 * g + 2)
                nc.vector.reciprocal(rrec[:, b, :], rsum[:, b, :]).then_inc(s_rec, 1)

            def coefficient(g, b):
                dve.wait_ge(s_rec, g + 1)
                nc.vector.tensor_tensor(coef[:, b, :], rrec[:, b, 1:2], lam[:, :], ALU.mult).then_inc(s_coef, 1)

            def combine(g, b, fresh):
                dve.wait_ge(s_e1, g + 1)
                dve.wait_ge(s_coef, g + 1)
                if not fresh:
                    dve.wait_ge(s_tr, g - 3)
                nc.vector.scalar_tensor_tensor(out=pm[:, b, :], in0=ex[:, b, 1, :], scalar=coef[:, b, :],
                                               in1=ex[:, b, 0, :], op0=ALU.mult, op1=ALU.add).then_inc(s_comb, 1)

            for n, what in enumerate(ORDER[:4]):
                low_part(0, 0, n // 2, what[0])

            def body(it, first, last):
                for t in range(2 * TPP):
                    j, st = t // TPP, t % TPP
                    g, pair = it * 2 * TPP + t, 2 * it + j
                    dve.wait_ge(s_score, g + 1)
                    nc.vector.tensor_reduce(nmax[:, t % 2, :], p_score[t % 2][:, :, :], AXX, ALU.max,
                                            negate=True).then_inc(s_max, 1)
                    if not (first and t < 1):
                        reciprocals(g - 1, (t - 1) % 4)
                    what = AT_STEP.get(st - 1)
                    if what and what[0] in "qk" and not (last and j == 1):
                        low_part(pair + 1, 1 - j, int(what[1]), what[0])
                    if not (first and t < 1):
                        coefficient(g - 1, (t - 1) % 4)
                    if not (first and t < 2):
                        combine(g - 2, (t - 2) % 4, first and t < 6)
                    if st == 0:
                        copy_v(pair, j, first)
            looped(dve, ITERS, body, peel_last=True)
            g = ITERS * 2 * TPP
            reciprocals(g - 1, 3)
            coefficient(g - 1, 3)
            combine(g - 2, 2, False)
            combine(g - 1, 3, False)

        @block.tensor
        def _(pe):
            def project(pair, j, what, fresh):
                n = ORDER.index(what)
                bank = p_proj[n % 2]
                if what == "q0" and not fresh:
                    pe.wait_ge(s_vT, pair)
                elif what == "k0" and not fresh:
                    pe.wait_ge(s_v, pair)
                elif what in ("q1", "k1", "v"):
                    pe.wait_ge(s_lo, 4 * pair + n - 1)
                if what == "vt":
                    pe.wait_ge(s_lo, 4 * pair + 4)
                    pe.wait_ge(s_vT, pair + 1)
                    for k in range(QT):
                        last_op = nc.tensor.transpose(bank[:, k * P:(k + 1) * P], vT[:, k * P:(k + 1) * P], ident)
                    last_op.then_inc(s_proj, 1)
                    return
                if what == "q0":
                    pe.wait_ge(s_w[j], 16 * (pair // 2 + 1))
                u = 0 if what == "v" else int(what[1])
                if what == "q0" and not fresh:
                    pe.wait_ge(s_xp, QT * (batch_of(pair) + 1))
                for k in range(KT):
                    for n, (a, b) in enumerate(((0, 0), (0, 1), (1, 0))):
                        x_part = xp[:, bass.ds(batch_of(pair) % 2, 1), b, k, :].rearrange("p a s -> p (a s)")
                        last_op = nc.tensor.matmul(bank[:, :], weights(j, a, what[0], u, k), x_part,
                                                   start=(k == 0 and n == 0), stop=(k == KT - 1 and n == 2))
                last_op.then_inc(s_proj, 1)

            def scores(g, j, st, pair, fresh):
                u, qt = st // QT, st % QT
                if qt == 0:
                    pe.wait_ge(s_dup[j][u], 16 * DUPS * (pair // 2 + 1))
                if not fresh:
                    pe.wait_ge(s_exp, 2 * g - 2)
                for m in range(2):
                    for part in range(2):
                        last_op = nc.tensor.matmul(p_score[st % 2][:, m, :],
                                                   qs[j][u][:, m, qt * P:(qt + 1) * P], ks[j][u][:, m, part, :],
                                                   start=(part == 0), stop=(part == 1))
                last_op.then_inc(s_score, 1)

            def transposes(g, a, fresh):
                pe.wait_ge(s_comb, g + 1)
                if not fresh:
                    pe.wait_ge(s_pT, g)
                for k in range(QT):
                    last_op = nc.tensor.transpose(p_tr[:, k, :], pm[:, a, k * P:(k + 1) * P], ident)
                last_op.then_inc(s_tr, 1)

            def times_v(pair, j, key_tiles, fresh):
                if key_tiles[0] == 0:
                    pe.wait_ge(s_pT, (pair + 1) * TPP)
                    pe.wait_ge(s_v, pair + 1)
                    if not fresh:
                        pe.wait_ge(s_o, pair)
                for k in key_tiles:
                    for u in range(2):
                        last_op = nc.tensor.matmul(p_pv[u * D:(u + 1) * D, :], v[j][:, k, u * D:(u + 1) * D],
                                                   pT[j][u][:, k, :], start=(k == 0), stop=(k == QT - 1))
                if key_tiles[-1] == QT - 1:
                    last_op.then_inc(s_pv, 1)

            for what in ORDER:
                project(0, 0, what, True)

            def body(it, first, last):
                for t in range(2 * TPP):
                    j, st = t // TPP, t % TPP
                    g, pair = it * 2 * TPP + t, 2 * it + j
                    scores(g, j, st, pair, first and t < 2)
                    if not (first and t < LAG):
                        transposes(g - LAG, (t - LAG) % 4, first and t == LAG)
                    if st in PV_STEP and not (first and j == 0):
                        times_v(pair - 1, 1 - j, PV_STEP[st], first)
                    what = AT_STEP.get(st)
                    if what and not (last and j == 1):
                        project(pair + 1, 1 - j, what, False)
            looped(pe, ITERS, body, peel_last=True)
            g = ITERS * 2 * TPP
            for t in range(LAG):
                transposes(g - LAG + t, (t - LAG) % 4, False)
            times_v(2 * ITERS - 1, 1, range(QT), False)


def ffn_stage(nc, ins, xn_d, token_d, ys_d, consts, tile_expert):
    with ExitStack() as ctx:
        def sb(name, shape, dt=F32):
            return ctx.enter_context(nc.sbuf_tensor(name, shape, dt))

        def ps(name, shape):
            return ctx.enter_context(nc.psum_tensor(name, shape, F32))

        def sem(name):
            return ctx.enter_context(nc.semaphore(name))

        w1 = [sb(f"w1_{j}", [P, KT, F]) for j in range(2)]
        w2 = [sb(f"w2_{j}", [P, FT, E]) for j in range(2)]
        b1 = [sb(f"b1_{j}", [P, FT]) for j in range(2)]
        b2 = [sb(f"b2_{j}", [P, E]) for j in range(2)]
        xs = [[sb(f"xs{j}{s}", [P, E]) for s in range(FS)] for j in range(2)]
        SC = SLOTS // P
        assert SC <= P
        token_rows = sb("token_rows", [SC, P])
        token = sb("slot_token", [P, SC], U32)
        s_rows, s_ttr, s_token = sem("f_rows"), sem("f_ttr"), sem("f_token")
        xsT = [sb(f"xsT{j}", [P, KT, FFN_TILE]) for j in range(2)]
        h = [sb(f"h{j}", [P, FT, FFN_TILE]) for j in range(2)]
        y = [sb(f"y{j}", [P, FS, E]) for j in range(2)]
        p_x = [ps(f"p_x{j}", [P, KT, FFN_TILE]) for j in range(2)]
        p_h = [ps(f"p_h{j}", [P, 2, FFN_TILE]) for j in range(2)]
        p_y = [ps(f"p_y{j}", [P, FS, E]) for j in range(2)]
        s_xs, s_w1 = [sem(f"f_xs{j}") for j in range(2)], [sem(f"f_w1{j}") for j in range(2)]
        s_w2, s_st = [sem(f"f_w2{j}") for j in range(2)], [sem(f"f_st{j}") for j in range(2)]
        s_tr, s_xT, s_h, s_gelu, s_y, s_yb = sem("f_tr"), sem("f_xT"), sem("f_h"), sem("f_gelu"), sem("f_y"), sem("f_yb")
        ident = consts[:, C_ID:C_ID + P]
        ys_v = ys_d.rearrange("(n s p) e -> n p s e", s=FS, p=P)
        HG = FT // 2
        LOOPED = FFN_TILES - 1
        assert LOOPED % 2 == 0

        def tiles_of(engine, body):
            body(0, 0, 0, True, True)
            body(1, 1, 0, False, True)
            body(2, 0, 1, False, False)
            with engine.Fori(1, LOOPED // 2) as i:
                body(2 * i + 1, 1, i, False, False)
                body(2 * i + 2, 0, i + 1, False, False)

        block = ctx.enter_context(nc.Block())

        @block.sync
        def _(sp):
            sp.dma_start(token_rows[:, :], token_d.rearrange("(c p) a -> c (p a)", p=P)).then_inc(s_rows, 16)

            def body(n, j, uses, first, fresh):
                e = sp.value_load(tile_expert[0:1, bass.ds(n, 1)], min_val=0, max_val=NE - 1)
                if not fresh:
                    sp.wait_ge(s_gelu, (n - 1) * FT)
                sp.dma_start(w1[j][:, :, :], ins["w1"][bass.ds(e, 1)].rearrange("a p k f -> (a p) k f")
                             ).then_inc(s_w1[j], 16)
                sp.dma_start(b1[j][:, :], ins["b1"][bass.ds(e, 1)].rearrange("a p f -> (a p) f")
                             ).then_inc(s_w1[j], 16)
                if not fresh:
                    sp.wait_ge(s_yb, n - 1)
                sp.dma_start(w2[j][:, :, :], ins["w2"][bass.ds(e, 1)].rearrange("a p k f -> (a p) k f")
                             ).then_inc(s_w2[j], 16)
                sp.dma_start(b2[j][:, :], ins["b2"][bass.ds(e, 1)].rearrange("a p f -> (a p) f")
                             ).then_inc(s_w2[j], 16)
            tiles_of(sp, body)

        @block.gpsimd
        def _(pool):
            pool.wait_ge(s_token, 1)

            def gather(n):
                j = n % 2
                if n >= 2:
                    pool.wait_ge(s_tr, n - 1)
                for s in range(FS):
                    c = n * FS + s
                    pool.indirect_dma_start(
                        out=xs[j][s][:, :], out_offset=None, in_=xn_d,
                        in_offset=bass.IndirectOffsetOnAxis(ap=token[:, c:c + 1], axis=0)
                    ).then_inc(s_xs[j], 16)

            gather(0)
            for n in range(FFN_TILES):
                if n + 1 < FFN_TILES:
                    gather(n + 1)
                pool.wait_ge(s_yb, n + 1)
                pool.dma_start(ys_v[n], y[n % 2][:, :, :]).then_inc(s_st[n % 2], 16)
            pool.wait_ge(s_st[0], 16 * (LOOPED // 2 + 1))
            pool.wait_ge(s_st[1], 16 * (LOOPED // 2))

        @block.scalar
        def _(act):
            def body(n, j, uses, first, fresh):
                act.wait_ge(s_w1[j], 32 * (uses + 1))
                if not fresh:
                    act.wait_ge(s_y, n - 1)
                for f in range(FT):
                    act.wait_ge(s_h, n * HG + f // 2 + 1)
                    nc.scalar.activation(h[j][:, f, :], p_h[(f // 2) % 2][:, f % 2, :], ACT.Gelu_apprx_tanh,
                                         bias=b1[j][:, f:f + 1]).then_inc(s_gelu, 1)
            tiles_of(act, body)

        @block.vector
        def _(dve):
            def body(n, j, uses, first, fresh):
                dve.wait_ge(s_tr, n + 1)
                if not fresh:
                    dve.wait_ge(s_h, (n - 1) * HG)
                nc.vector.tensor_copy(xsT[j][:, :, :], p_x[j][:, :, :]).then_inc(s_xT, 1)
                if not first:
                    add_b2(n - 1, 1 - j, uses if j == 1 else uses - 1, fresh)

            def add_b2(n, j, uses, fresh):
                dve.wait_ge(s_y, n + 1)
                dve.wait_ge(s_w2[j], 32 * (uses + 1))
                if not fresh:
                    dve.wait_ge(s_st[j], 16 * uses)
                nc.vector.tensor_tensor(y[j][:, :, :], p_y[j][:, :, :],
                                        b2[j][:, :].unsqueeze(1).to_broadcast([P, FS, E]), ALU.add
                                        ).then_inc(s_yb, 1)
            dve.wait_ge(s_ttr, 1)
            nc.vector.tensor_copy(token[:, :], p_y[1][:, 0, 0:SC]).then_inc(s_token, 1)
            body(0, 0, 0, True, True)
            body(1, 1, 0, False, True)
            dve.wait_ge(s_tr, 3)
            dve.wait_ge(s_h, HG)
            nc.vector.tensor_copy(xsT[0][:, :, :], p_x[0][:, :, :]).then_inc(s_xT, 1)
            add_b2(1, 1, 0, True)
            with dve.Fori(1, LOOPED // 2) as i:
                body(2 * i + 1, 1, i, False, False)
                body(2 * i + 2, 0, i + 1, False, False)
            add_b2(FFN_TILES - 1, 0, LOOPED // 2, False)

        @block.tensor
        def _(pe):
            def transposes(n, j, uses, fresh):
                pe.wait_ge(s_xs[j], 16 * FS * (uses + 1))
                if not fresh:
                    pe.wait_ge(s_xT, n - 1)
                for k in range(KT):
                    for s in range(FS):
                        last_op = nc.tensor.transpose(p_x[j][:, k, s * P:(s + 1) * P],
                                                      xs[j][s][:, k * P:(k + 1) * P], ident)
                last_op.then_inc(s_tr, 1)

            def body(n, j, uses, first, fresh, last=False):
                pe.wait_ge(s_xT, n + 1)
                pe.wait_ge(s_w1[j], 32 * (uses + 1))
                for g in range(HG):
                    if not (first and g < 2):
                        pe.wait_ge(s_gelu, (n * HG + g - 1) * 2)
                    for f in range(2 * g, 2 * g + 2):
                        for k in range(KT):
                            last_op = nc.tensor.matmul(p_h[g % 2][:, f % 2, :], w1[j][:, k, f * P:(f + 1) * P],
                                                       xsT[j][:, k, :], start=(k == 0), stop=(k == KT - 1))
                    last_op.then_inc(s_h, 1)
                if not last:
                    transposes(n + 1, 1 - j, (uses if j == 0 else uses + 1), first)
                pe.wait_ge(s_w2[j], 32 * (uses + 1))
                pe.wait_ge(s_gelu, (n + 1) * FT)
                if not fresh:
                    pe.wait_ge(s_yb, n - 1)
                for s in range(FS):
                    for f in range(FT):
                        last_op = nc.tensor.matmul(p_y[j][:, s, :], h[j][:, f, s * P:(s + 1) * P], w2[j][:, f, :],
                                                   start=(f == 0), stop=(f == FT - 1))
                last_op.then_inc(s_y, 1)

            pe.wait_ge(s_rows, 16)
            nc.tensor.transpose(p_y[1][:, 0, 0:SC], token_rows[:, :], ident[0:SC, 0:SC]).then_inc(s_ttr, 1)
            transposes(0, 0, 0, True)
            body(0, 0, 0, True, True)
            body(1, 1, 0, False, True)
            body(2, 0, 1, False, False)
            with pe.Fori(1, LOOPED // 2 - 1) as i:
                body(2 * i + 1, 1, i, False, False)
                body(2 * i + 2, 0, i + 1, False, False)
            i = LOOPED // 2 - 1
            body(2 * i + 1, 1, i, False, False)
            body(2 * i + 2, 0, i + 1, False, False, last=True)


def output_stage(nc, ins, oT_d, ys_d, slot_u, prob, out):
    G = 2 * P
    with ExitStack() as ctx:
        def sb(name, shape, dt=F32):
            return ctx.enter_context(nc.sbuf_tensor(name, shape, dt))

        def sem(name):
            return ctx.enter_context(nc.semaphore(name))

        wo = sb("wo", [P, PAIRS, E])
        rows = sb("rows", [P, 3, E])
        oTs = [sb(f"oTs{j}", [P, PAIRS, G]) for j in range(2)]
        x = [sb(f"x{j}", [P, 2, E]) for j in range(2)]
        ff = [[sb(f"ff{j}{s}", [P, E]) for s in range(2)] for j in range(2)]
        yb, yn = [sb(f"yb{j}", [P, 2, E]) for j in range(2)], [sb(f"yn{j}", [P, 2, E]) for j in range(2)]
        acc = [sb(f"acc{j}", [P, 2, E]) for j in range(2)]
        stats, mom = sb("ostats", [P, 2, 6]), sb("omom", [P, 6, 2])
        s_root = sem("o_root")
        p_y = [ctx.enter_context(nc.psum_tensor(f"po{j}", [P, 2, E], F32)) for j in range(2)]
        s_c, s_sc = sem("o_c"), sem("o_sc")
        s_o, s_x = [sem(f"o_o{j}") for j in range(2)], [sem(f"o_x{j}") for j in range(2)]
        s_ff, s_st = [sem(f"o_ff{j}") for j in range(2)], [sem(f"o_st{j}") for j in range(2)]
        s_y, s_d, s_res, s_out = sem("o_y"), sem("o_d"), sem("o_res"), sem("o_out")
        steps = T // G // 2
        DVE_STEPS = MOMENT_STEPS + 5
        x_v = ins["x"].rearrange("(n s p) e -> n p s e", s=2, p=P)
        out_v = out.rearrange("(n s p) e -> n p s e", s=2, p=P)
        oT_v = oT_d.rearrange("h p t -> p h t")
        bro = [P, 2, E]

        def row(i):
            return rows[:, i, :].unsqueeze(1).to_broadcast(bro)

        block = ctx.enter_context(nc.Block())

        @block.sync
        def _(sp):
            sp.dma_start(wo[:, :, :], ins["wo"]).then_inc(s_c, 16)
            sp.dma_start(rows[:, :, :], ins["out_rows"]).then_inc(s_c, 16)

            def load(n, j, fresh):
                if not fresh:
                    sp.wait_ge(s_y, n - 1)
                sp.dma_start(oTs[j][:, :, :], oT_v[:, :, bass.ds(n * G, G)]).then_inc(s_o[j], 16)
                if not fresh:
                    sp.wait_ge(s_res, n - 1)
                sp.dma_start(x[j][:, :, :], x_v[bass.ds(n, 1)].rearrange("a p s e -> (a p) s e")
                             ).then_inc(s_x[j], 16)

            def store(n, j):
                sp.wait_ge(s_out, 2 * n + 2)
                sp.dma_start(out_v[bass.ds(n, 1)].rearrange("a p s e -> (a p) s e"), acc[j][:, :, :]
                             ).then_inc(s_st[j], 16)

            load(0, 0, True)
            load(1, 1, True)

            def body(i, first, last):
                for j in range(2):
                    n = 2 * i + j
                    store(n, j)
                    if not last:
                        load(n + 2, j, False)
            looped(sp, steps, body, peel_last=True)
            for j in range(2):
                sp.wait_ge(s_st[j], 16 * steps)

        @block.gpsimd
        def _(pool):
            for n in range(2 * steps):
                j = n % 2
                if n >= 2:
                    pool.wait_ge(s_out, 2 * n - 2)
                for s in range(2):
                    c = 2 * n + s
                    pool.indirect_dma_start(
                        out=ff[j][s][:, :], out_offset=None, in_=ys_d,
                        in_offset=bass.IndirectOffsetOnAxis(ap=slot_u[:, c:c + 1], axis=0)
                    ).then_inc(s_ff[j], 16)

        @block.scalar
        def _(act):
            def body(i, first, last):
                for j in range(2):
                    act.wait_ge(s_d, DVE_STEPS * (2 * i + j) + 2 + RECIPROCAL_STEP)
                    nc.scalar.activation(mom[:, 5, :], mom[:, 4, :], ACT.Sqrt).then_inc(s_root, 1)
            looped(act, steps, body)

        @block.tensor
        def _(pe):
            pe.wait_ge(s_c, 32)

            def body(i, first, last):
                for j in range(2):
                    n = 2 * i + j
                    pe.wait_ge(s_o[j], 16 * (i + 1))
                    if not first:
                        pe.wait_ge(s_d, DVE_STEPS * (n - 2) + 1)
                    for s in range(2):
                        for k in range(PAIRS):
                            last_op = nc.tensor.matmul(p_y[j][:, s, :], oTs[j][:, k, s * P:(s + 1) * P], wo[:, k, :],
                                                       start=(k == 0), stop=(k == PAIRS - 1))
                    last_op.then_inc(s_y, 1)
            looped(pe, steps, body)

        @block.vector
        def _(dve):
            v = nc.vector
            dve.wait_ge(s_c, 32)
            v.tensor_scalar(rows[:, 1:3, :], rows[:, 1:3, :], OUT_SCALE, None, ALU.mult).then_inc(s_sc, 1)
            dve.wait_ge(s_sc, 1)

            def body(i, first, last):
                for j in range(2):
                    n = 2 * i + j
                    done = [0]

                    def step(ins_):
                        done[0] += 1
                        ins_.then_inc(s_d, 1)
                        dve.wait_ge(s_d, DVE_STEPS * n + done[0])

                    dve.wait_ge(s_y, n + 1)
                    step(v.tensor_tensor(yb[j][:, :, :], p_y[j][:, :, :], row(0), ALU.add))
                    for s in range(2):
                        last_op = v.bn_stats(stats[:, s, :], yb[j][:, s, :])
                    step(last_op)
                    moments(nc, dve, step, stats, mom, s_root, n + 1)
                    for s in range(2):
                        last_op = v.tensor_scalar(yn[j][:, s, :], yb[j][:, s, :], mom[:, 0, s:s + 1], mom[:, 1, s:s + 1],
                                                  ALU.subtract, ALU.mult)
                    step(last_op)
                    step(v.tensor_tensor(yn[j][:, :, :], yn[j][:, :, :], row(1), ALU.mult))
                    step(v.tensor_tensor(yn[j][:, :, :], yn[j][:, :, :], row(2), ALU.add))
                    dve.wait_ge(s_x[j], 16 * (i + 1))
                    v.tensor_tensor(yn[j][:, :, :], yn[j][:, :, :], x[j][:, :, :], ALU.add).then_inc(s_res, 1)
                    dve.wait_ge(s_res, n + 1)
                    dve.wait_ge(s_ff[j], 32 * (i + 1))
                    if not first:
                        dve.wait_ge(s_st[j], 16 * i)
                    for s in range(2):
                        v.scalar_tensor_tensor(out=acc[j][:, s, :], in0=ff[j][s][:, :],
                                               scalar=prob[:, bass.ds(2 * n + s, 1)], in1=yn[j][:, s, :],
                                               op0=ALU.mult, op1=ALU.add).then_inc(s_out, 1)
            looped(dve, steps, body)


def build(nc, ins, out):
    wp_d = nc.dram_tensor("weight_parts_scratch", [PAIRS, P, 2, WPAIR], F32).ap()
    xn_d = nc.dram_tensor("xn_scratch", [T, E], F32).ap()
    token_d = nc.dram_tensor("token_scratch", [SLOTS, 1], F32).ap()
    ys_d = nc.dram_tensor("ys_scratch", [SLOTS, E], F32).ap()
    oT_d = nc.dram_tensor("oT_scratch", [PAIRS, P, T], F32).ap()
    with ExitStack() as ctx:
        def sb(name, shape, dt=F32):
            return ctx.enter_context(nc.sbuf_tensor(name, shape, dt))

        consts = sb("consts", [P, CONSTS])
        slot_u, prob = sb("slot_u", [P, NT], U32), sb("prob", [P, NT])
        tile_expert = sb("tile_expert", [P, FFN_TILES], I32)
        with ExitStack() as att:
            xT = att.enter_context(nc.sbuf_tensor("xT", [P, KT, T], F32))
            xp = att.enter_context(nc.sbuf_tensor("xp", [P, 2, 2, KT, S], F32R))
            w = [att.enter_context(nc.sbuf_tensor(f"w{j}", [P, 2, WPAIR], F32R)) for j in range(2)]
            with ExitStack() as routing:
                sw = routing.enter_context(nc.sbuf_tensor("sw", [P, KT, NE], F32))
                pL = routing.enter_context(nc.psum_tensor("pL", [P, 512], F32))
                norm_stage(nc, ins, wp_d, xn_d, xT, consts, sw, pL)
                route_stage(nc, ins, wp_d, token_d, xT, xp, w, consts, pL, slot_u, prob, tile_expert)
            attention_stage(nc, ins, wp_d, token_d, oT_d, xT, xp, w, consts, slot_u)
        ffn_stage(nc, ins, xn_d, token_d, ys_d, consts, tile_expert)
        output_stage(nc, ins, oT_d, ys_d, slot_u, prob, out)


def kernel(L0_attn_X, L0_attn_Wq, L0_attn_bq, L0_attn_Wk, L0_attn_bk, L0_attn_Wv, L0_attn_bv, L0_attn_Wo,
           L0_attn_bo, L0_attn_gamma, L0_attn_beta, L0_attn_lam, L0_ffn_switch_w, L0_ffn_switch_b,
           L0_ffn_w1, L0_ffn_b1, L0_ffn_w2, L0_ffn_b2):
    import concourse.bacc as bacc
    import numpy as np
    from concourse.bass_utils import run_bass_kernel_spmd

    def a(x):
        return np.asarray(x)

    def wide(x):
        x = a(x)
        return np.broadcast_to(x[None], (P,) + x.shape)

    def by_pair(wt, width):
        return a(wt).reshape(PAIRS, 2, KT, P, width).transpose(0, 3, 2, 1, 4).reshape(PAIRS, P, KT * 2 * width)

    idx = np.arange(P)
    consts = np.concatenate([
        np.eye(P), idx[:, None] < idx[None, :],
        np.broadcast_to(np.arange(MAXT) * FFN_TILE, (P, MAXT)),
        np.broadcast_to(np.arange(FFN_TILES), (P, FFN_TILES)),
        idx[:, None] + P * np.arange(NT)[None]], axis=1).astype(np.float32)
    arrays = {
        "x": a(L0_attn_X).reshape(T, E),
        "consts": consts,
        "sw": a(L0_ffn_switch_w).reshape(KT, P, NE).transpose(1, 0, 2),
        "swb": wide(L0_ffn_switch_b),
        "w_attn": np.concatenate([by_pair(L0_attn_Wq, 2 * D), by_pair(L0_attn_Wk, 2 * D),
                                  by_pair(L0_attn_Wv, D)], axis=2),
        "attn_bias": np.concatenate([a(L0_attn_bq).T.reshape(P, PAIRS, 2), a(L0_attn_bk).T.reshape(P, PAIRS, 2),
                                     a(L0_attn_bv).reshape(PAIRS, P).T[:, :, None]], axis=2),
        "lam": np.broadcast_to(a(L0_attn_lam).reshape(1, 1), (P, 1)),
        "w1": a(L0_ffn_w1).reshape(NE, KT, P, F).transpose(0, 2, 1, 3),
        "w2": a(L0_ffn_w2).reshape(NE, FT, P, E).transpose(0, 2, 1, 3),
        "b1": a(L0_ffn_b1).reshape(NE, FT, P).transpose(0, 2, 1),
        "b2": np.broadcast_to(a(L0_ffn_b2)[:, None, :], (NE, P, E)),
        "wo": a(L0_attn_Wo).reshape(PAIRS, P, E).transpose(1, 0, 2),
        "out_rows": np.stack([wide(L0_attn_bo), wide(L0_attn_gamma), wide(L0_attn_beta)], axis=1),
    }
    arrays = {k: np.ascontiguousarray(x) for k, x in arrays.items()}
    nc = bacc.Bacc("TRN2", target_bir_lowering=False, num_devices=1)
    ins = {k: nc.dram_tensor("in_" + k, x.shape, F32, kind="ExternalInput").ap() for k, x in arrays.items()}
    out = nc.dram_tensor("out", [T, E], F32, kind="ExternalOutput").ap()
    build(nc, ins, out)
    r = run_bass_kernel_spmd(nc, [{"in_" + k: x for k, x in arrays.items()}], core_ids=[0])
    return r.results[0]["out"].reshape(B, S, E)
```

```python
from contextlib import ExitStack

import concourse.bass as bass
from concourse import mybir

F32 = mybir.dt.float32
F32R = mybir.dt.float32r
I32 = mybir.dt.int32
U32 = mybir.dt.uint32
ALU = mybir.AluOpType
ACT = mybir.ActivationFunctionType
AXX = mybir.AxisListType.X

P = 128
B, S, E = 8, 512, 256
H, D = 16, 64
T = B * S
NT = T // P
KT = E // P
EPS = 1e-5
SCALE = float(D) ** -0.5
OUT_SCALE = 1.0 - 0.8
NE, F = 8, 1024
FT = F // P
FFN_TILE = 256
FFN_TILES = (T + NE * (FFN_TILE - 1)) // FFN_TILE
SLOTS = FFN_TILES * FFN_TILE
FS = FFN_TILE // P
MAXT = T // FFN_TILE
PAIRS = H // 2
QT = S // P
TPP = 2 * QT
ITERS = B * PAIRS // 2
WPAIR = KT * (2 * P + 2 * P + 2 * D)
C_ID, C_UP, C_J, C_T = 0, P, 2 * P, 2 * P + MAXT
C_TOKEN = C_T + FFN_TILES
CONSTS = C_TOKEN + NT


def looped(engine, count, body, peel_last=False):
    body(0, True, False)
    end = count - 1 if peel_last else count
    with engine.Fori(1, end) as turn:
        body(turn, False, False)
    if peel_last:
        body(count - 1, False, True)


MOMENT_STEPS, RECIPROCAL_STEP = 9, 5


def moments(nc, dve, step, stats, mom, s_root, roots):
    v = nc.vector
    mean, rstd, dif, ve, rec, root = (mom[:, k, :] for k in range(6))
    v.tensor_tensor(mean, stats[:, :, 1], stats[:, :, 4], ALU.add)
    v.tensor_tensor(dif, stats[:, :, 1], stats[:, :, 4], ALU.subtract)
    step(v.tensor_tensor(ve, stats[:, :, 2], stats[:, :, 5], ALU.add))
    v.tensor_scalar(mean, mean, 0.5, None, ALU.mult)
    v.tensor_scalar(dif, dif, 0.5, None, ALU.mult)
    step(v.tensor_scalar(ve, ve, 1.0 / E, EPS, ALU.mult, ALU.add))
    step(v.tensor_tensor(dif, dif, dif, ALU.mult))
    step(v.tensor_tensor(ve, ve, dif, ALU.add))
    step(v.reciprocal(rec, ve))
    dve.wait_ge(s_root, roots)
    step(v.tensor_tensor(dif, root, root, ALU.mult))
    step(v.tensor_tensor(dif, dif, ve, ALU.mult))
    step(v.tensor_scalar(dif, dif, -0.5, 1.5, ALU.mult, ALU.add))
    step(v.tensor_tensor(rstd, root, dif, ALU.mult))


class WeightParts:

    def __init__(self, nc, ctx, ins, wp_d, name, first_pair, count, buffers):
        def sem(what):
            return ctx.enter_context(nc.semaphore(f"{name}_{what}"))

        self.nc, self.w_d, self.wp_d, self.first_pair, self.count = nc, ins["w_attn"], wp_d, first_pair, count
        self.buffers = buffers
        self.w = [ctx.enter_context(nc.sbuf_tensor(f"{name}_w{b}", [P, WPAIR], F32)) for b in range(buffers)]
        self.parts = [ctx.enter_context(nc.sbuf_tensor(f"{name}_parts{b}", [P, 2, WPAIR], F32R))
                      for b in range(buffers)]
        self.s_w = [sem(f"w{b}") for b in range(buffers)]
        self.s_stored = [sem(f"stored{b}") for b in range(buffers)]
        self.s_scaled, self.s_high, self.s_low = sem("scaled"), sem("high"), sem("low")

    def load(self, sp, k, b):
        src = self.w_d[bass.ds(self.first_pair + k, 1)].rearrange("c p n -> (c p) n")
        sp.dma_start(self.w[b][:, :], src).then_inc(self.s_w[b], 16)

    def sync(self, sp, k, b, last):
        sp.wait_ge(self.s_low, k + 1)
        if not last:
            self.load(sp, k + self.buffers, b)
        dst = self.wp_d[bass.ds(self.first_pair + k, 1)].rearrange("c p a n -> (c p) a n")
        sp.dma_start(dst, self.parts[b][:, :, :].bitcast(F32)).then_inc(self.s_stored[b], 16)

    def scalar(self, act, k, b, uses, fresh):
        act.wait_ge(self.s_w[b], 16 * (uses + 1))
        wq = self.w[b][:, 0:KT * 2 * P]
        self.nc.scalar.activation(wq, wq, ACT.Identity, scale=SCALE).then_inc(self.s_scaled, 1)
        act.wait_ge(self.s_scaled, k + 1)
        if not fresh:
            act.wait_ge(self.s_stored[b], 16 * uses)
        self.nc.scalar.copy(self.parts[b][:, 0, :], self.w[b][:, :]).then_inc(self.s_high, 1)

    def gpsimd(self, pool, k, b):
        pool.wait_ge(self.s_high, k + 1)
        self.nc.gpsimd.tensor_tensor(self.parts[b][:, 1, :], self.w[b][:, :], self.parts[b][:, 0, :].bitcast(F32),
                                     ALU.subtract).then_inc(self.s_low, 1)

    def finish(self, sp):
        for b in range(self.buffers):
            sp.wait_ge(self.s_stored[b], 16 * (self.count // self.buffers))


def norm_stage(nc, ins, wp_d, xn_d, xT, consts, sw, pL):
    G = 2 * P
    TURN = 4
    TURNS = T // G // TURN
    with ExitStack() as ctx:
        def sb(name, shape, dt=F32):
            return ctx.enter_context(nc.sbuf_tensor(name, shape, dt))

        def sem(name):
            return ctx.enter_context(nc.semaphore(name))

        xin = [sb(f"xin{j}", [P, 2, E]) for j in range(TURN)]
        xn = [sb(f"xn{j}", [P, 2, E]) for j in range(TURN)]
        xt = [sb(f"xt{a}", [P, KT, G]) for a in range(2)]
        stats, mom = sb("stats", [P, 2 * TURN, 6]), sb("mom", [P, 6, 2 * TURN])
        wparts = WeightParts(nc, ctx, ins, wp_d, "n_wt", 0, TURNS, 1)
        pX = [ctx.enter_context(nc.psum_tensor(f"pX{a}", [P, KT, G], F32)) for a in range(2)]
        s_const = sem("n_const")
        s_x = [sem(f"n_x{j}") for j in range(TURN)]
        s_store = [sem(f"n_store{j}") for j in range(TURN)]
        s_stat, s_d, s_root, s_xn = sem("n_stat"), sem("n_dve"), sem("n_root"), sem("n_xn")
        s_tr, s_xt, s_logit = sem("n_tr"), sem("n_xt"), sem("n_logit")
        x_d = ins["x"].rearrange("(n s p) e -> n p s e", s=2, p=P)
        xn_v = xn_d.rearrange("(n s p) e -> n p s e", s=2, p=P)

        def at(ap, n):
            return ap[bass.ds(n, 1)].rearrange("a p s e -> (a p) s e")

        block = ctx.enter_context(nc.Block())

        @block.sync
        def _(sp):
            for j in range(TURN):
                sp.dma_start(xin[j][:, :, :], at(x_d, j)).then_inc(s_x[j], 16)
            sp.dma_start(consts[:, :], ins["consts"]).then_inc(s_const, 16)
            sp.dma_start(sw[:, :, :], ins["sw"]).then_inc(s_const, 16)
            wparts.load(sp, 0, 0)

            def body(i, first, last):
                for j in range(TURN):
                    n = TURN * i + j
                    sp.wait_ge(s_xn, n + 1)
                    if not last:
                        sp.dma_start(xin[j][:, :, :], at(x_d, n + TURN)).then_inc(s_x[j], 16)
                    sp.dma_start(at(xn_v, n), xn[j][:, :, :]).then_inc(s_store[j], 16)
                wparts.sync(sp, i, 0, last)
            looped(sp, TURNS, body, peel_last=True)
            for j in range(TURN):
                sp.wait_ge(s_store[j], 16 * TURNS)
            wparts.finish(sp)

        @block.gpsimd
        def _(pool):
            looped(pool, TURNS, lambda i, first, last: wparts.gpsimd(pool, i, 0))

        @block.vector
        def _(dve):
            def body(i, first, last):
                done = [0]

                def step(ins_):
                    done[0] += 1
                    ins_.then_inc(s_d, 1)
                    dve.wait_ge(s_d, MOMENT_STEPS * i + done[0])

                for j in range(TURN):
                    dve.wait_ge(s_x[j], 16 * (i + 1))
                    for s in range(2):
                        nc.vector.bn_stats(stats[:, 2 * j + s, :], xin[j][:, s, :]).then_inc(s_stat, 1)
                dve.wait_ge(s_stat, 2 * TURN * (i + 1))
                moments(nc, dve, step, stats, mom, s_root, i + 1)
                for j in range(TURN):
                    n = TURN * i + j
                    if not first:
                        dve.wait_ge(s_tr, n - TURN + 1)
                        dve.wait_ge(s_store[j], 16 * i)
                    for s in range(2):
                        a = 2 * j + s
                        last_op = nc.vector.tensor_scalar(xn[j][:, s, :], xin[j][:, s, :], mom[:, 0, a:a + 1],
                                                          mom[:, 1, a:a + 1], ALU.subtract, ALU.mult)
                    last_op.then_inc(s_xn, 1)
            looped(dve, TURNS, body)

        @block.scalar
        def _(act):
            def root(i):
                act.wait_ge(s_d, MOMENT_STEPS * i + RECIPROCAL_STEP)
                nc.scalar.activation(mom[:, 5, :], mom[:, 4, :], ACT.Sqrt).then_inc(s_root, 1)

            def body(i, first, last):
                for j in range(TURN):
                    n, a = TURN * i + j, j % 2
                    if j == 2:
                        wparts.scalar(act, i, 0, i, first)
                    act.wait_ge(s_tr, n + 1)
                    if not (first and j < 2):
                        act.wait_ge(s_logit, n - 1)
                    nc.scalar.copy(xt[a][:, :, :], pX[a][:, :, :])
                    nc.scalar.copy(xT[:, :, bass.ds(n * G, G)], pX[a][:, :, :]).then_inc(s_xt, 1)
                    if j == 1 and not last:
                        root(i + 1)
            root(0)
            looped(act, TURNS, body, peel_last=True)

        @block.tensor
        def _(pe):
            pe.wait_ge(s_const, 32)
            ident = consts[:, C_ID:C_ID + P]

            def body(i, first, last):
                for j in range(TURN):
                    n, a = TURN * i + j, j % 2
                    pe.wait_ge(s_xn, n + 1)
                    if not (first and j < 2):
                        pe.wait_ge(s_xt, n - 1)
                    for k in range(KT):
                        for s in range(2):
                            last_op = nc.tensor.transpose(pX[a][:, k, s * P:(s + 1) * P],
                                                          xn[j][:, s, k * P:(k + 1) * P], ident)
                    last_op.then_inc(s_tr, 1)
                    if not (first and j == 0):
                        logits(n - 1, 1 - a)

            def logits(n, a):
                pe.wait_ge(s_xt, n + 1)
                for s in range(2):
                    for k in range(KT):
                        last_op = nc.tensor.matmul(pL[:, bass.ds((n * 2 + s) * NE, NE)],
                                                   xt[a][:, k, s * P:(s + 1) * P], sw[:, k, :],
                                                   start=(k == 0), stop=(k == KT - 1))
                last_op.then_inc(s_logit, 1)

            looped(pe, TURNS, body)
            logits(TURNS * TURN - 1, 1)


def route_stage(nc, ins, wp_d, token_d, xT, xp, w_first, consts, pL, slot_u, prob, tile_expert):
    with ExitStack() as ctx:
        def sb(name, shape, dt=F32):
            return ctx.enter_context(nc.sbuf_tensor(name, shape, dt))

        def sem(name):
            return ctx.enter_context(nc.semaphore(name))

        swb, weight = sb("swb", [P, NE]), sb("weight", [P, NE])
        lg, ex, oh = sb("lg", [P, NT, NE]), sb("ex", [P, NT, NE]), sb("oh", [P, NT, NE])
        col, den = sb("col", [P, NT]), sb("den", [P, NT])
        inc, exc = sb("inc", [P, NE, NT]), sb("exc", [P, NE, NT])
        ones, upper = sb("ones", [P, P]), consts[:, C_UP:C_UP + P]
        more = sb("more", [P, NE, MAXT])
        tiles, tile_end, base = sb("tiles", [P, NE]), sb("tile_end", [P, NE]), sb("base", [P, NE])
        slot_f = sb("slot_f", [P, NT])
        past, te_f = sb("past", [P, FFN_TILES, NE]), sb("te_f", [P, FFN_TILES])
        pR = ctx.enter_context(nc.psum_tensor("pR", [P, NT, NE], F32))
        pC = ctx.enter_context(nc.psum_tensor("pC", [P, NT, NE], F32))
        wparts = WeightParts(nc, ctx, ins, wp_d, "r_wt", PAIRS // 2, PAIRS // 2, 2)
        no_token = sb("no_token", [P, SLOTS // P])
        s_zero, s_zeroed, s_xhi, s_xlo, s_wfirst = (
            sem("r_zero"), sem("r_zeroed"), sem("r_xhi"), sem("r_xlo"), sem("r_wfirst"))
        x_parts = [xp[:, 0, part, :, :] for part in range(2)]
        s_in, s_d, s_e, s_rank, s_p = sem("r_in"), sem("r_dve"), sem("r_exp"), sem("r_rank"), sem("r_pool")
        block = ctx.enter_context(nc.Block())
        SHIFTED, ONEHOT = 3, 9

        @block.sync
        def _(sp):
            sp.dma_start(swb[:, :], ins["swb"]).then_inc(s_in, 16)
            for b in range(2):
                wparts.load(sp, b, b)
            for j in range(2):
                sp.dma_start(w_first[j][:, :, :].bitcast(F32), wp_d[j]).then_inc(s_wfirst, 16)
            sp.wait_ge(s_zero, 1)
            sp.dma_start(token_d.rearrange("(p n) a -> p (n a)", p=P), no_token[:, :]).then_inc(s_zeroed, 16)
            for k in range(wparts.count):
                wparts.sync(sp, k, k % 2, k >= wparts.count - 2)
            wparts.finish(sp)
            sp.wait_ge(s_wfirst, 32)
            sp.wait_ge(s_zeroed, 16)

        @block.gpsimd
        def _(pool):
            nc.gpsimd.memset(ones[:, :], 1.0).then_inc(s_p, 1)
            for e in range(NE):
                last_op = nc.gpsimd.memset(weight[:, e:e + 1], float(NE - e))
            last_op.then_inc(s_p, 1)
            nc.gpsimd.memset(no_token[:, :], 0.0).then_inc(s_zero, 1)
            pool.wait_ge(s_xhi, 1)
            nc.gpsimd.tensor_tensor(x_parts[1], xT[:, :, 0:S], x_parts[0].bitcast(F32), ALU.subtract
                                    ).then_inc(s_xlo, 1)
            for k in range(wparts.count):
                wparts.gpsimd(pool, k, k % 2)

        @block.scalar
        def _(act):
            nc.scalar.copy(x_parts[0], xT[:, :, 0:S]).then_inc(s_xhi, 1)
            act.wait_ge(s_d, SHIFTED)
            nc.scalar.activation(ex[:, :, :], lg[:, :, :], ACT.Exp).then_inc(s_e, 1)
            for k in range(wparts.count):
                wparts.scalar(act, k, k % 2, k // 2, k < 2)

        @block.tensor
        def _(pe):
            pe.wait_ge(s_p, 2)
            pe.wait_ge(s_d, ONEHOT)
            nc.tensor.matmul(pR[:, :, :], upper, oh[:, :, :], start=True, stop=True)
            nc.tensor.matmul(pC[:, :, :], ones[:, :], oh[:, :, :], start=True, stop=True).then_inc(s_rank, 1)

        @block.vector
        def _(dve):
            done = [0]

            def step(ins_):
                done[0] += 1
                ins_.then_inc(s_d, 1)
                dve.wait_ge(s_d, done[0])

            tne, v = [P, NT, NE], nc.vector
            pLv = pL[:, 0:NT * NE].rearrange("p (t e) -> p t e", e=NE)
            dve.wait_ge(s_in, 16)
            step(v.tensor_tensor(lg[:, :, :], pLv, swb[:, :].unsqueeze(1).to_broadcast(tne), ALU.add))
            step(v.tensor_reduce(col[:, :], lg[:, :, :], AXX, ALU.max))
            step(v.tensor_tensor(lg[:, :, :], lg[:, :, :], col[:, :].unsqueeze(2).to_broadcast(tne), ALU.subtract))
            dve.wait_ge(s_p, 2)
            dve.wait_ge(s_e, 1)
            step(v.tensor_reduce(den[:, :], ex[:, :, :], AXX, ALU.add))
            step(v.reciprocal(prob[:, :], den[:, :]))
            step(v.tensor_scalar(oh[:, :, :], lg[:, :, :], 0.0, None, ALU.is_equal))
            step(v.tensor_tensor(ex[:, :, :], oh[:, :, :], weight[:, :].unsqueeze(1).to_broadcast(tne), ALU.mult))
            step(v.tensor_reduce(col[:, :], ex[:, :, :], AXX, ALU.max))
            step(v.tensor_tensor(oh[:, :, :], ex[:, :, :], col[:, :].unsqueeze(2).to_broadcast(tne), ALU.is_equal))
            dve.wait_ge(s_rank, 1)
            cnt = pC[:, :, :].rearrange("p t e -> p e t")
            for e in range(NE):
                last_op = v.tensor_tensor_scan(inc[:, e, :], ones[:, 0:NT], cnt[:, e, :], 0.0, ALU.mult, ALU.add)
            step(last_op)
            step(v.tensor_tensor(exc[:, :, :], inc[:, :, :], cnt, ALU.subtract))
            em = [P, NE, MAXT]
            step(v.tensor_tensor(more[:, :, :], inc[:, :, NT - 1:NT].to_broadcast(em),
                                 consts[:, C_J:C_J + MAXT].unsqueeze(1).to_broadcast(em), ALU.is_gt))
            step(v.tensor_reduce(tiles[:, :], more[:, :, :], AXX, ALU.add))
            step(v.tensor_tensor_scan(tile_end[:, :], ones[:, 0:NE], tiles[:, :], 0.0, ALU.mult, ALU.add))
            step(v.tensor_tensor(base[:, :], tile_end[:, :], tiles[:, :], ALU.subtract))
            step(v.tensor_scalar(base[:, :], base[:, :], float(FFN_TILE), None, ALU.mult))
            step(v.tensor_tensor(lg[:, :, :], pR[:, :, :], exc[:, :, :].rearrange("p e t -> p t e"), ALU.add))
            step(v.tensor_tensor(lg[:, :, :], lg[:, :, :], base[:, :].unsqueeze(1).to_broadcast(tne), ALU.add))
            step(v.tensor_tensor(lg[:, :, :], lg[:, :, :], oh[:, :, :], ALU.mult))
            step(v.tensor_reduce(slot_f[:, :], lg[:, :, :], AXX, ALU.add))
            step(v.tensor_copy(slot_u[:, :], slot_f[:, :]))
            fe = [P, FFN_TILES, NE]
            step(v.tensor_tensor(past[:, :, :], tile_end[:, :].unsqueeze(1).to_broadcast(fe),
                                 consts[:, C_T:C_T + FFN_TILES].unsqueeze(2).to_broadcast(fe), ALU.is_le))
            step(v.tensor_reduce(te_f[:, :], past[:, :, :], AXX, ALU.add))
            step(v.tensor_scalar(te_f[:, :], te_f[:, :], float(NE - 1), None, ALU.min))
            step(v.tensor_copy(tile_expert[:, :], te_f[:, :]))


def attention_stage(nc, ins, wp_d, token_d, oT_d, xT, xp, w, consts, slot_u):
    with ExitStack() as ctx:
        def sb(name, shape, dt=F32):
            return ctx.enter_context(nc.sbuf_tensor(name, shape, dt))

        def ps(name, shape):
            return ctx.enter_context(nc.psum_tensor(name, shape, F32))

        def sem(name):
            return ctx.enter_context(nc.semaphore(name))

        bias = sb("bias", [P, PAIRS, 5])
        bias_of = {"q": 0, "k": 2, "v": 4}
        bias_now = [sb(f"bias_now{j}", [P, 5]) for j in range(2)]
        lam = sb("lam", [P, 1])
        parts = {"q": [sb(f"q_parts{u}", [P, 2, S], F32R) for u in range(2)],
                 "k": [sb(f"k_parts{u}", [P, 2, S], F32R) for u in range(2)]}
        qs = [[sb(f"qs{j}{u}", [P, 2, S], F32R) for u in range(2)] for j in range(2)]
        ks = [[sb(f"ks{j}{u}", [P, 2, 2, S], F32R) for u in range(2)] for j in range(2)]
        vT = sb("vT", [P, S])
        v = [sb(f"v{j}", [P, QT, P]) for j in range(2)]
        ex = sb("e", [P, 4, 2, S])
        pm = sb("pm", [P, 4, S])
        pT = [[sb(f"pT{j}{u}", [P, QT, S]) for u in range(2)] for j in range(2)]
        oT = [sb(f"oT{j}", [P, S]) for j in range(2)]
        nmax = sb("nmax", [P, 2, 2])
        rsum, rrec, coef = sb("rsum", [P, 4, 2]), sb("rrec", [P, 4, 2]), sb("coef", [P, 4, 1])
        token, token_slot = sb("token", [P, 1]), sb("token_slot", [P, 1], U32)
        p_score = [ps(f"p_score{a}", [P, 2, S]) for a in range(2)]
        p_tr, p_pv = ps("p_tr", [P, QT, P]), ps("p_pv", [P, S])
        p_proj = [ps(f"p_proj{a}", [P, S]) for a in range(2)]

        s_const, s_w, s_dup = sem("a_const"), [sem(f"a_w{j}") for j in range(2)], \
            [[sem(f"a_dup{j}{u}") for u in range(2)] for j in range(2)]
        s_xhi, s_xp, s_bias = sem("a_xhi"), sem("a_xp"), sem("a_bias")
        s_proj, s_hi, s_lo, s_vT, s_v = sem("a_proj"), sem("a_hi"), sem("a_lo"), sem("a_vT"), sem("a_v")
        s_score, s_max, s_exp = sem("a_score"), sem("a_max"), sem("a_exp")
        s_rec, s_coef, s_e1, s_comb = sem("a_rec"), sem("a_coef"), sem("a_e1"), sem("a_comb")
        s_tr, s_pT, s_pv, s_o = sem("a_tr"), sem("a_pT"), sem("a_pv"), sem("a_o")
        s_ost = [sem(f"a_ost{j}") for j in range(2)]
        s_idx, s_scat, s_lam, s_bq = sem("a_idx"), sem("a_scat"), sem("a_lam"), sem("a_bq")

        ident = consts[:, C_ID:C_ID + P]
        LAG = 4
        DUPS = 8

        ORDER = ("q0", "k0", "q1", "k1", "v", "vt")
        AT_STEP = {0: "q0", 1: "k0", 2: "q1", 3: "k1", 4: "v", 6: "vt"}
        PV_STEP = {5: (0,), 6: (1,), 7: (2, 3)}

        def batch_of(pair):
            return pair // PAIRS

        def weights(j, part, what, u, k):
            if what == "v":
                return w[j][:, part, KT * 4 * P + k * P:KT * 4 * P + (k + 1) * P]
            o = (0 if what == "q" else KT * 2 * P) + k * 2 * P + u * P
            return w[j][:, part, o:o + P]

        block = ctx.enter_context(nc.Block())

        @block.sync
        def _(sp):
            sp.dma_start(bias[:, :, :], ins["attn_bias"]).then_inc(s_const, 16)
            sp.dma_start(lam[:, :], ins["lam"]).then_inc(s_const, 16)
            for j in range(2):
                sp.nop().then_inc(s_ost[j], 16)
                sp.nop().then_inc(s_w[j], 16)

            def load_w(pair, j):
                src = wp_d[bass.ds(pair % PAIRS, 1)].rearrange("a p c n -> (a p) c n")
                sp.dma_start(w[j][:, :, :].bitcast(F32), src).then_inc(s_w[j], 16)

            def spread(j, u, what, pair):
                n = 4 * pair + 2 * u + (what == "k")
                sp.wait_ge(s_lo, n + 1)
                src = parts[what][u]
                for m in range(2):
                    a = src[m * D:(m + 1) * D]
                    if what == "q":
                        for part in range(2):
                            sp.dma_start(qs[j][u][part * D:(part + 1) * D, m, :].bitcast(F32),
                                         a[:, part, :].bitcast(F32)).then_inc(s_dup[j][u], 16)
                    else:
                        for half in range(2):
                            sp.dma_start(ks[j][u][half * D:(half + 1) * D, m, :, :].bitcast(F32),
                                         a[:, :, :].bitcast(F32)).then_inc(s_dup[j][u], 16)

            for u in range(2):
                for what in "qk":
                    spread(0, u, what, 0)

            def body(it, first, last):
                for j in range(2):
                    pair = 2 * it + j
                    nj = 1 - j
                    if not last:
                        sp.wait_ge(s_proj, 6 * pair + 5)
                        load_w(pair + 2, j)
                    if not (last and j == 1):
                        for u in range(2):
                            for what in "qk":
                                spread(nj, u, what, pair + 1)
                    if not first:
                        store_o(pair - 2, j)

            def store_o(pair, j):
                sp.wait_ge(s_o, pair + 1)
                dst = oT_d[bass.ds(pair % PAIRS, 1), :, bass.ds(batch_of(pair) * S, S)]
                sp.dma_start(dst.rearrange("a p n -> (a p) n"), oT[j][:, :]).then_inc(s_ost[j], 16)

            looped(sp, ITERS, body, peel_last=True)
            store_o(2 * ITERS - 2, 0)
            store_o(2 * ITERS - 1, 1)
            for j in range(2):
                sp.wait_ge(s_ost[j], 16 * (ITERS + 1))

        @block.gpsimd
        def _(pool):
            def pair_bias(pair, j):
                nc.gpsimd.tensor_copy(bias_now[j][:, :], bias[:, bass.ds(pair % PAIRS, 1), :]
                                      .rearrange("p a c -> p (a c)")).then_inc(s_bias, 1)

            pool.wait_ge(s_bq, 1)
            pair_bias(0, 0)
            pair_bias(1, 1)
            pool.nop().then_inc(s_xp, QT)

            def split_x(quarter):
                cols = bass.ds(quarter % (T // P) * P, P)
                place = (quarter // QT) % 2, quarter % QT
                hi, lo = (xp[:, bass.ds(place[0], 1), part, :, bass.ds(place[1] * P, P)]
                          .rearrange("p a k s -> p (a k) s") for part in range(2))
                nc.gpsimd.tensor_copy(hi, xT[:, :, cols]).then_inc(s_xhi, 1)
                pool.wait_ge(s_xhi, quarter - QT + 1)
                nc.gpsimd.tensor_tensor(lo, xT[:, :, cols], hi.bitcast(F32), ALU.subtract).then_inc(s_xp, 1)

            def body(it, first, last):
                if not first:
                    pool.wait_ge(s_scat, 16 * it)
                nc.gpsimd.tensor_copy(token_slot[:, :], slot_u[:, bass.ds(it, 1)])
                nc.gpsimd.tensor_copy(token[:, :], consts[:, bass.ds(C_TOKEN + it, 1)]).then_inc(s_idx, 1)
                for t in range(2 * TPP):
                    g = it * 2 * TPP + t
                    if t == 2:
                        pool.wait_ge(s_idx, it + 1)
                    pool.wait_ge(s_rec, g + 1)
                    e1 = ex[:, t % 4, 0, :]
                    nc.gpsimd.tensor_tensor(e1, e1, rrec[:, t % 4, 0:1].to_broadcast([P, S]), ALU.mult
                                            ).then_inc(s_e1, 1)
                    if t == 0:
                        pool.wait_ge(s_proj, 6 * 2 * it + 6)
                        split_x(it + QT)
                    if t % TPP == 5 and not last:
                        pair = 2 * it + t // TPP
                        pool.wait_ge(s_lo, 4 * pair + 4)
                        pool.wait_ge(s_vT, pair + 1)
                        pair_bias(pair + 2, t // TPP)
                    if t == 2:
                        pool.indirect_dma_start(
                            out=token_d, out_offset=bass.IndirectOffsetOnAxis(ap=token_slot[:, 0:1], axis=0),
                            in_=token[:, :], in_offset=None).then_inc(s_scat, 16)
            looped(pool, ITERS, body, peel_last=True)
            pool.wait_ge(s_scat, 16 * ITERS)

        @block.scalar
        def _(act):
            def high_part(pair, j, u, what, fresh=False):
                n = 4 * pair + 2 * u + (what == "k")
                act.wait_ge(s_proj, 6 * pair + ORDER.index(f"{what}{u}") + 1)
                if not fresh:
                    act.wait_ge(s_dup[1 - j][u], 16 * DUPS * ((pair - 1) // 2 + 1))
                if (what, u) == ("q", 0):
                    act.wait_ge(s_bias, pair + 1)
                b = bias_now[j][:, bias_of[what] + u:bias_of[what] + u + 1]
                nc.scalar.activation(parts[what][u][:, 0, :], p_proj[n % 2][:, :],
                                     ACT.Identity, bias=b).then_inc(s_hi, 1)

            def v_bias(pair, j):
                act.wait_ge(s_proj, 6 * pair + 5)
                b = bias_now[j][:, bias_of["v"]:bias_of["v"] + 1]
                nc.scalar.activation(vT[:, :], p_proj[0][:, :], ACT.Identity, bias=b).then_inc(s_vT, 1)

            def copy_pT(g, j, u, qt, pair, fresh):
                act.wait_ge(s_tr, g + 1)
                if u == qt == 0 and not fresh:
                    act.wait_ge(s_pv, pair - 1)
                nc.scalar.copy(pT[j][u][:, :, qt * P:(qt + 1) * P], p_tr[:, :, :]).then_inc(s_pT, 1)

            def copy_o(pair, j):
                act.wait_ge(s_pv, pair + 1)
                act.wait_ge(s_ost[j], 16 * (pair // 2 + 1))
                nc.scalar.copy(oT[j][:, :], p_pv[:, :]).then_inc(s_o, 1)

            for n, what in enumerate(ORDER[:4]):
                high_part(0, 0, n // 2, what[0], True)
            v_bias(0, 0)

            def body(it, first, last):
                for t in range(2 * TPP):
                    j, st = t // TPP, t % TPP
                    g, pair = it * 2 * TPP + t, 2 * it + j
                    if st == 0 and not first:
                        copy_o(pair - 2, j)
                    what = AT_STEP.get(st - 1)
                    if what and not (last and j == 1):
                        if what[0] in "qk":
                            high_part(pair + 1, 1 - j, int(what[1]), what[0])
                        elif what == "v":
                            v_bias(pair + 1, 1 - j)
                    if not (first and t < LAG):
                        lt = (t - LAG) % (2 * TPP)
                        lj, lst = lt // TPP, lt % TPP
                        lpair = pair if t % TPP >= LAG else pair - 1
                        copy_pT(g - LAG, lj, lst // QT, lst % QT, lpair, first)
                    for m in range(2):
                        act.wait_ge(s_max, g + 1)
                        if m == 0 and not (first and t < 4):
                            act.wait_ge(s_comb, g - 3)
                        nc.scalar.activation(ex[:, t % 4, m, :], p_score[t % 2][:, m, :], ACT.Exp,
                                             bias=nmax[:, t % 2, m:m + 1],
                                             accum_out=rsum[:, t % 4, m:m + 1]).then_inc(s_exp, 1)
            looped(act, ITERS, body, peel_last=True)
            g = ITERS * 2 * TPP
            for t in range(LAG):
                lst = TPP - LAG + t
                copy_pT(g - LAG + t, 1, lst // QT, lst % QT, 2 * ITERS - 1, False)
            copy_o(2 * ITERS - 2, 0)
            copy_o(2 * ITERS - 1, 1)

        @block.vector
        def _(dve):
            dve.wait_ge(s_const, 32)
            nc.vector.tensor_scalar(bias[:, :, 0:2], bias[:, :, 0:2], SCALE, None, ALU.mult).then_inc(s_bq, 1)
            nc.vector.tensor_scalar(lam[:, :], lam[:, :], -1.0, None, ALU.mult).then_inc(s_lam, 1)
            dve.wait_ge(s_bq, 1)
            dve.wait_ge(s_lam, 1)

            def low_part(pair, j, u, what):
                n = 4 * pair + 2 * u + (what == "k")
                dve.wait_ge(s_hi, n + 1)
                if (what, u) == ("q", 0):
                    dve.wait_ge(s_bias, pair + 1)
                b = bias_now[j][:, bias_of[what] + u:bias_of[what] + u + 1]
                nc.vector.scalar_tensor_tensor(out=parts[what][u][:, 1, :], in0=p_proj[n % 2][:, :], scalar=b,
                                               in1=parts[what][u][:, 0, :].bitcast(F32),
                                               op0=ALU.add, op1=ALU.subtract).then_inc(s_lo, 1)

            def copy_v(pair, j, fresh):
                dve.wait_ge(s_proj, 6 * pair + 6)
                if not fresh:
                    dve.wait_ge(s_pv, pair - 1)
                nc.vector.tensor_copy(v[j][:, :, :], p_proj[1][:, :].rearrange("p (k d) -> p k d", d=P)
                                      ).then_inc(s_v, 1)

            def reciprocals(g, b):
                dve.wait_ge(s_exp, 2 * g + 2)
                nc.vector.reciprocal(rrec[:, b, :], rsum[:, b, :]).then_inc(s_rec, 1)

            def coefficient(g, b):
                dve.wait_ge(s_rec, g + 1)
                nc.vector.tensor_tensor(coef[:, b, :], rrec[:, b, 1:2], lam[:, :], ALU.mult).then_inc(s_coef, 1)

            def combine(g, b, fresh):
                dve.wait_ge(s_e1, g + 1)
                dve.wait_ge(s_coef, g + 1)
                if not fresh:
                    dve.wait_ge(s_tr, g - 3)
                nc.vector.scalar_tensor_tensor(out=pm[:, b, :], in0=ex[:, b, 1, :], scalar=coef[:, b, :],
                                               in1=ex[:, b, 0, :], op0=ALU.mult, op1=ALU.add).then_inc(s_comb, 1)

            for n, what in enumerate(ORDER[:4]):
                low_part(0, 0, n // 2, what[0])

            def body(it, first, last):
                for t in range(2 * TPP):
                    j, st = t // TPP, t % TPP
                    g, pair = it * 2 * TPP + t, 2 * it + j
                    dve.wait_ge(s_score, g + 1)
                    nc.vector.tensor_reduce(nmax[:, t % 2, :], p_score[t % 2][:, :, :], AXX, ALU.max,
                                            negate=True).then_inc(s_max, 1)
                    if not (first and t < 1):
                        reciprocals(g - 1, (t - 1) % 4)
                    what = AT_STEP.get(st - 1)
                    if what and what[0] in "qk" and not (last and j == 1):
                        low_part(pair + 1, 1 - j, int(what[1]), what[0])
                    if not (first and t < 1):
                        coefficient(g - 1, (t - 1) % 4)
                    if not (first and t < 2):
                        combine(g - 2, (t - 2) % 4, first and t < 6)
                    if st == 0:
                        copy_v(pair, j, first)
            looped(dve, ITERS, body, peel_last=True)
            g = ITERS * 2 * TPP
            reciprocals(g - 1, 3)
            coefficient(g - 1, 3)
            combine(g - 2, 2, False)
            combine(g - 1, 3, False)

        @block.tensor
        def _(pe):
            def project(pair, j, what, fresh):
                n = ORDER.index(what)
                bank = p_proj[n % 2]
                if what == "q0" and not fresh:
                    pe.wait_ge(s_vT, pair)
                elif what == "k0" and not fresh:
                    pe.wait_ge(s_v, pair)
                elif what in ("q1", "k1", "v"):
                    pe.wait_ge(s_lo, 4 * pair + n - 1)
                if what == "vt":
                    pe.wait_ge(s_lo, 4 * pair + 4)
                    pe.wait_ge(s_vT, pair + 1)
                    for k in range(QT):
                        last_op = nc.tensor.transpose(bank[:, k * P:(k + 1) * P], vT[:, k * P:(k + 1) * P], ident)
                    last_op.then_inc(s_proj, 1)
                    return
                if what == "q0":
                    pe.wait_ge(s_w[j], 16 * (pair // 2 + 1))
                u = 0 if what == "v" else int(what[1])
                if what == "q0" and not fresh:
                    pe.wait_ge(s_xp, QT * (batch_of(pair) + 1))
                for k in range(KT):
                    for n, (a, b) in enumerate(((0, 0), (0, 1), (1, 0))):
                        x_part = xp[:, bass.ds(batch_of(pair) % 2, 1), b, k, :].rearrange("p a s -> p (a s)")
                        last_op = nc.tensor.matmul(bank[:, :], weights(j, a, what[0], u, k), x_part,
                                                   start=(k == 0 and n == 0), stop=(k == KT - 1 and n == 2))
                last_op.then_inc(s_proj, 1)

            def scores(g, j, st, pair, fresh):
                u, qt = st // QT, st % QT
                if qt == 0:
                    pe.wait_ge(s_dup[j][u], 16 * DUPS * (pair // 2 + 1))
                if not fresh:
                    pe.wait_ge(s_exp, 2 * g - 2)
                for m in range(2):
                    for part in range(2):
                        last_op = nc.tensor.matmul(p_score[st % 2][:, m, :],
                                                   qs[j][u][:, m, qt * P:(qt + 1) * P], ks[j][u][:, m, part, :],
                                                   start=(part == 0), stop=(part == 1))
                last_op.then_inc(s_score, 1)

            def transposes(g, a, fresh):
                pe.wait_ge(s_comb, g + 1)
                if not fresh:
                    pe.wait_ge(s_pT, g)
                for k in range(QT):
                    last_op = nc.tensor.transpose(p_tr[:, k, :], pm[:, a, k * P:(k + 1) * P], ident)
                last_op.then_inc(s_tr, 1)

            def times_v(pair, j, key_tiles, fresh):
                if key_tiles[0] == 0:
                    pe.wait_ge(s_pT, (pair + 1) * TPP)
                    pe.wait_ge(s_v, pair + 1)
                    if not fresh:
                        pe.wait_ge(s_o, pair)
                for k in key_tiles:
                    for u in range(2):
                        last_op = nc.tensor.matmul(p_pv[u * D:(u + 1) * D, :], v[j][:, k, u * D:(u + 1) * D],
                                                   pT[j][u][:, k, :], start=(k == 0), stop=(k == QT - 1))
                if key_tiles[-1] == QT - 1:
                    last_op.then_inc(s_pv, 1)

            for what in ORDER:
                project(0, 0, what, True)

            def body(it, first, last):
                for t in range(2 * TPP):
                    j, st = t // TPP, t % TPP
                    g, pair = it * 2 * TPP + t, 2 * it + j
                    scores(g, j, st, pair, first and t < 2)
                    if not (first and t < LAG):
                        transposes(g - LAG, (t - LAG) % 4, first and t == LAG)
                    if st in PV_STEP and not (first and j == 0):
                        times_v(pair - 1, 1 - j, PV_STEP[st], first)
                    what = AT_STEP.get(st)
                    if what and not (last and j == 1):
                        project(pair + 1, 1 - j, what, False)
            looped(pe, ITERS, body, peel_last=True)
            g = ITERS * 2 * TPP
            for t in range(LAG):
                transposes(g - LAG + t, (t - LAG) % 4, False)
            times_v(2 * ITERS - 1, 1, range(QT), False)


def ffn_stage(nc, ins, xn_d, token_d, ys_d, oT_d, consts, tile_expert, pre):
    with ExitStack() as ctx:
        def sb(name, shape, dt=F32):
            return ctx.enter_context(nc.sbuf_tensor(name, shape, dt))

        def ps(name, shape):
            return ctx.enter_context(nc.psum_tensor(name, shape, F32))

        def sem(name):
            return ctx.enter_context(nc.semaphore(name))

        HG = FT // 2
        SC = SLOTS // P
        assert SC <= P
        w1 = [sb(f"w1_{j}", [P, KT, F]) for j in range(2)]
        w2 = [sb(f"w2_{j}", [P, FT, E]) for j in range(2)]
        w1p = [sb(f"w1p_{j}", [P, 2, KT, F], F32R) for j in range(2)]
        w2p = [sb(f"w2p_{j}", [P, 2, FT, E], F32R) for j in range(2)]
        b1 = [sb(f"b1_{j}", [P, FT]) for j in range(2)]
        b2 = [sb(f"b2_{j}", [P, E]) for j in range(2)]
        xs = [[sb(f"xs{j}{s}", [P, E]) for s in range(FS)] for j in range(2)]
        xsp = [sb(f"xsp{j}", [P, 2, KT, FFN_TILE], F32R) for j in range(2)]
        h = sb("h", [P, HG, 2, FFN_TILE])
        hp = [sb(f"hp{j}", [P, 2, FT, FFN_TILE], F32R) for j in range(2)]
        y = [sb(f"y{j}", [P, FS, E]) for j in range(2)]
        token_rows = sb("token_rows", [SC, P])
        token = sb("slot_token", [P, SC], U32)
        p_x = [ps(f"p_x{j}", [P, KT, FFN_TILE]) for j in range(2)]
        p_h = [ps(f"p_h{a}", [P, 2, FFN_TILE]) for a in range(2)]
        p_y = [ps(f"p_y{j}", [P, FS, E]) for j in range(2)]

        def sems(name):
            return [sem(f"{name}{j}") for j in range(2)]

        s_xs, s_w1, s_w2, s_b1, s_b2, s_st = (sems(f"f_{x}") for x in ("xs", "w1", "w2", "b1", "b2", "st"))
        s_pre = sem("f_pre")
        s_rows, s_ttr, s_token = sem("f_rows"), sem("f_ttr"), sem("f_token")
        s_tr, s_h, s_gelu, s_y, s_yb = sem("f_tr"), sem("f_h"), sem("f_gelu"), sem("f_y"), sem("f_yb")
        s_xhi, s_xlo, s_hhi, s_hlo = sem("f_xhi"), sem("f_xlo"), sem("f_hhi"), sem("f_hlo")
        s_w1hi, s_w1lo, s_w2hi, s_w2lo = sem("f_w1hi"), sem("f_w1lo"), sem("f_w2hi"), sem("f_w2lo")
        ident = consts[:, C_ID:C_ID + P]
        ys_v = ys_d.rearrange("(n s p) e -> n p s e", s=FS, p=P)
        THREE = ((0, 0), (0, 1), (1, 0))
        LOOPED = FFN_TILES - 1
        assert LOOPED % 2 == 0 and LOOPED >= 6

        class Turn:

            def __init__(self, n, j, half, exact):
                self.n, self.j, self.half, self.exact = n, j, half, exact
                self.half_next = half + 1 if j == 1 else half
                self.half_before = half - 1 if j == 0 else half

            def after(self, k):
                return self.n >= k if self.exact else True

            def has(self, k):
                return self.n + k < FFN_TILES if self.exact else True

        def turns(body):
            def run(engine):
                for n in range(3):
                    body(Turn(n, n % 2, n // 2, True))
                with engine.Fori(1, LOOPED // 2 - 1) as i:
                    body(Turn(2 * i + 1, 1, i, False))
                    body(Turn(2 * i + 2, 0, i + 1, False))
                for n in (FFN_TILES - 2, FFN_TILES - 1):
                    body(Turn(n, n % 2, n // 2, True))
            return run

        block = ctx.enter_context(nc.Block())

        @block.sync
        def _(sp):
            sp.dma_start(token_rows[:, :], token_d.rearrange("(c p) a -> c (p a)", p=P)).then_inc(s_rows, 16)

            def expert(n):
                return sp.value_load(tile_expert[0:1, bass.ds(n, 1)], min_val=0, max_val=NE - 1)

            def load(dst, j, name, e, signal):
                src = ins[name][bass.ds(e, 1)]
                if len(dst.shape) == 3:
                    sp.dma_start(dst[:, :, :], src.rearrange("a p k f -> (a p) k f")).then_inc(signal[j], 16)
                else:
                    sp.dma_start(dst[:, :], src.rearrange("a p f -> (a p) f")).then_inc(signal[j], 16)

            e = expert(0)
            load(w1[0], 0, "w1", e, s_w1)
            load(b1[0], 0, "b1", e, s_b1)
            load(w2[0], 0, "w2", e, s_w2)
            load(b2[0], 0, "b2", e, s_b2)
            e = expert(1)
            load(w1[1], 1, "w1", e, s_w1)
            load(b1[1], 1, "b1", e, s_b1)

            def body(t):
                n, j = t.n, t.j
                if t.has(2):
                    e2 = expert(n + 2)
                    sp.wait_ge(s_w1lo, KT * (n + 1))
                    load(w1[j], j, "w1", e2, s_w1)
                if t.has(1):
                    e1 = expert(n + 1)
                    if t.after(1):
                        sp.wait_ge(s_w2lo, n)
                    load(w2[1 - j], 1 - j, "w2", e1, s_w2)
                if t.has(2):
                    sp.wait_ge(s_gelu, (n + 1) * FT)
                    load(b1[j], j, "b1", e2, s_b1)
                if t.after(1):
                    store(n - 1, 1 - j)
                if t.has(1):
                    load(b2[1 - j], 1 - j, "b2", e1, s_b2)

            def store(n, j):
                sp.wait_ge(s_yb, n + 1)
                sp.dma_start(ys_v[bass.ds(n, 1)].rearrange("a p s e -> (a p) s e"), y[j][:, :, :]
                             ).then_inc(s_st[j], 16)

            sp.dma_start(pre["wo"][:, :, :], ins["wo"]).then_inc(s_pre, 16)
            sp.dma_start(pre["rows"][:, :, :], ins["out_rows"]).then_inc(s_pre, 16)
            for c in range(2):
                sp.dma_start(pre["oTs"][c][:, :, :], oT_d.rearrange("h p t -> p h t")[:, :, c * 2 * P:(c + 1) * 2 * P]
                             ).then_inc(s_pre, 16)
            for n in range(4):
                sp.dma_start(pre["x"][n][:, :, :], ins["x"].rearrange("(n s p) e -> n p s e", s=2, p=P)[n]
                             ).then_inc(s_pre, 16)

            turns(body)(sp)
            store(FFN_TILES - 1, 0)
            sp.wait_ge(s_pre, 16 * 8)
            sp.wait_ge(s_st[0], 16 * (LOOPED // 2 + 1))
            sp.wait_ge(s_st[1], 16 * (LOOPED // 2))

        @block.gpsimd
        def _(pool):
            pool.wait_ge(s_token, 1)

            def gather(n):
                if n >= 2:
                    pool.wait_ge(s_tr, n - 1)
                for s in range(FS):
                    c = n * FS + s
                    pool.indirect_dma_start(
                        out=xs[n % 2][s][:, :], out_offset=None, in_=xn_d,
                        in_offset=bass.IndirectOffsetOnAxis(ap=token[:, c:c + 1], axis=0)
                    ).then_inc(s_xs[n % 2], 16)

            gather(0)
            gather(1)
            for n in range(FFN_TILES):
                if n + 2 < FFN_TILES:
                    gather(n + 2)
                pool.wait_ge(s_w2hi, n + 1)
                j = n % 2
                nc.gpsimd.tensor_tensor(w2p[j][:, 1, :, :], w2[j][:, :, :], w2p[j][:, 0, :, :].bitcast(F32),
                                        ALU.subtract).then_inc(s_w2lo, 1)

        @block.scalar
        def _(act):
            def x_high(n, j, fresh):
                act.wait_ge(s_tr, n + 1)
                if not fresh:
                    act.wait_ge(s_h, HG * (n - 1))
                nc.scalar.copy(xsp[j][:, 0, :, :], p_x[j][:, :, :]).then_inc(s_xhi, 1)

            x_high(0, 0, True)

            def body(t):
                n, j = t.n, t.j
                act.wait_ge(s_b1[j], 16 * (t.half + 1))
                if t.after(2):
                    act.wait_ge(s_y, n - 1)
                for g in range(HG):
                    act.wait_ge(s_h, n * HG + g + 1)
                    if t.after(1):
                        act.wait_ge(s_hlo, HG * (n - 1) + g + 1)
                    for c in range(2):
                        f = 2 * g + c
                        nc.scalar.activation(h[:, g, c, :], p_h[g % 2][:, c, :], ACT.Gelu_apprx_tanh,
                                             bias=b1[j][:, f:f + 1]).then_inc(s_gelu, 1)
                    act.wait_ge(s_gelu, n * FT + 2 * g + 2)
                    nc.scalar.copy(hp[j][:, 0, 2 * g:2 * g + 2, :], h[:, g, :, :]).then_inc(s_hhi, 1)
                if t.has(1):
                    x_high(n + 1, 1 - j, not t.after(1))
                act.wait_ge(s_w2[j], 16 * (t.half + 1))
                nc.scalar.copy(w2p[j][:, 0, :, :], w2[j][:, :, :]).then_inc(s_w2hi, 1)
            turns(body)(act)

        @block.vector
        def _(dve):
            v = nc.vector
            dve.wait_ge(s_ttr, 1)
            v.tensor_copy(token[:, :], p_y[1][:, 0, 0:SC]).then_inc(s_token, 1)

            def x_low(n, j):
                dve.wait_ge(s_xhi, n + 1)
                v.tensor_tensor(xsp[j][:, 1, :, :], p_x[j][:, :, :], xsp[j][:, 0, :, :].bitcast(F32),
                                ALU.subtract).then_inc(s_xlo, 1)

            def w1_high(n, j, half, k, fresh):
                if k == 0:
                    dve.wait_ge(s_w1[j], 16 * (half + 1))
                    if not fresh:
                        dve.wait_ge(s_h, HG * (n - 1))
                v.tensor_copy(w1p[j][:, 0, k, :], w1[j][:, k, :]).then_inc(s_w1hi, 1)

            def w1_low(n, j, k):
                dve.wait_ge(s_w1hi, KT * n + k + 1)
                v.tensor_tensor(w1p[j][:, 1, k, :], w1[j][:, k, :], w1p[j][:, 0, k, :].bitcast(F32),
                                ALU.subtract).then_inc(s_w1lo, 1)

            def add_b2(n, j, half, fresh):
                dve.wait_ge(s_y, n + 1)
                dve.wait_ge(s_b2[j], 16 * (half + 1))
                if not fresh:
                    dve.wait_ge(s_st[j], 16 * half)
                v.tensor_tensor(y[j][:, :, :], p_y[j][:, :, :], b2[j][:, :].unsqueeze(1).to_broadcast([P, FS, E]),
                                ALU.add).then_inc(s_yb, 1)

            for k in range(KT):
                w1_high(0, 0, 0, k, True)
            for k in range(KT):
                w1_low(0, 0, k)
            x_low(0, 0)

            def body(t):
                n, j = t.n, t.j
                for g in range(HG):
                    dve.wait_ge(s_hhi, n * HG + g + 1)
                    if g == 0 and t.after(2):
                        dve.wait_ge(s_y, n - 1)
                    v.tensor_tensor(hp[j][:, 1, 2 * g:2 * g + 2, :], h[:, g, :, :],
                                    hp[j][:, 0, 2 * g:2 * g + 2, :].bitcast(F32), ALU.subtract).then_inc(s_hlo, 1)
                    if t.has(1):
                        if g < KT:
                            w1_high(n + 1, 1 - j, t.half_next, g, not t.after(1))
                        else:
                            w1_low(n + 1, 1 - j, g - KT)
                if t.has(1):
                    x_low(n + 1, 1 - j)
                if t.after(1):
                    add_b2(n - 1, 1 - j, t.half_before, not t.after(3))
            assert HG == 2 * KT
            turns(body)(dve)
            add_b2(FFN_TILES - 1, 0, LOOPED // 2, False)

        @block.tensor
        def _(pe):
            def transposes(n, j, half, fresh):
                pe.wait_ge(s_xs[j], 16 * FS * (half + 1))
                if not fresh:
                    pe.wait_ge(s_xlo, n - 1)
                for k in range(KT):
                    for s in range(FS):
                        last_op = nc.tensor.transpose(p_x[j][:, k, s * P:(s + 1) * P],
                                                      xs[j][s][:, k * P:(k + 1) * P], ident)
                last_op.then_inc(s_tr, 1)

            def hidden(t):
                n, j = t.n, t.j
                pe.wait_ge(s_xlo, n + 1)
                pe.wait_ge(s_w1lo, KT * (n + 1))
                for g in range(HG):
                    if t.after(1) or g >= 2:
                        pe.wait_ge(s_gelu, (n * HG + g - 1) * 2)
                    for f in range(2 * g, 2 * g + 2):
                        for k in range(KT):
                            for c, (a, b) in enumerate(THREE):
                                last_op = nc.tensor.matmul(
                                    p_h[g % 2][:, f % 2, :], w1p[j][:, a, k, f * P:(f + 1) * P], xsp[j][:, b, k, :],
                                    start=(k == 0 and c == 0), stop=(k == KT - 1 and c == 2))
                    last_op.then_inc(s_h, 1)

            def outputs(n, j, fresh):
                pe.wait_ge(s_w2lo, n + 1)
                pe.wait_ge(s_hlo, HG * (n + 1))
                if not fresh:
                    pe.wait_ge(s_yb, n - 1)
                for s in range(FS):
                    for f in range(FT):
                        for c, (a, b) in enumerate(THREE):
                            last_op = nc.tensor.matmul(
                                p_y[j][:, s, :], hp[j][:, a, f, s * P:(s + 1) * P], w2p[j][:, b, f, :],
                                start=(f == 0 and c == 0), stop=(f == FT - 1 and c == 2))
                last_op.then_inc(s_y, 1)

            pe.wait_ge(s_rows, 16)
            nc.tensor.transpose(p_y[1][:, 0, 0:SC], token_rows[:, :], ident[0:SC, 0:SC]).then_inc(s_ttr, 1)
            transposes(0, 0, 0, True)

            def body(t):
                hidden(t)
                if t.has(1):
                    transposes(t.n + 1, 1 - t.j, t.half_next, not t.after(1))
                if t.after(1):
                    outputs(t.n - 1, 1 - t.j, not t.after(3))
            turns(body)(pe)
            outputs(FFN_TILES - 1, 0, False)


def output_stage(nc, ins, oT_d, ys_d, slot_u, prob, pre, out):
    G = 2 * P
    GROUPS, R = T // G, 4
    TURNS = GROUPS // R
    with ExitStack() as ctx:
        def sb(name, shape, dt=F32):
            return ctx.enter_context(nc.sbuf_tensor(name, shape, dt))

        def sem(name):
            return ctx.enter_context(nc.semaphore(name))

        wo, rows, oTs, x = pre["wo"], pre["rows"], pre["oTs"], pre["x"]
        gamma, beta = rows[:, 1, :], rows[:, 2, :]
        wop = sb("wop", [P, 2, PAIRS, E], F32R)
        bop = sb("bop", [1, 2, E], F32R)
        ones, ones_r = sb("out_ones", [1, P]), sb("ones_r", [1, P], F32R)
        op = [sb(f"op{c}", [P, 2, PAIRS, G], F32R) for c in range(2)]
        yn = [sb(f"yn{r}", [P, 2, E]) for r in range(R)]
        ff = [[sb(f"ff{r}{s}", [P, E]) for s in range(2)] for r in range(R)]
        acc = [sb(f"acc{r}", [P, 2, E]) for r in range(R)]
        stats = [sb(f"ostats{a}", [P, 4, 6]) for a in range(2)]
        mom, shift = [sb(f"omom{a}", [P, 6, 4]) for a in range(2)], [sb(f"shift{a}", [P, 4]) for a in range(2)]
        p_y = [ctx.enter_context(nc.psum_tensor(f"po{r}", [P, 2, E], F32)) for r in range(R)]
        s_ones, s_scaled, s_hi, s_lo = sem("o_ones"), sem("o_scaled"), sem("o_hi"), sem("o_lo")
        s_o = [sem(f"o_o{c}") for c in range(2)]
        s_x, s_ff, s_st = ([sem(f"o_{w}{r}") for r in range(R)] for w in ("x", "ff", "st"))
        s_ohi, s_olo, s_y, s_bn, s_d = sem("o_ohi"), sem("o_olo"), sem("o_y"), sem("o_bn"), sem("o_d")
        s_root, s_norm, s_xb, s_gamma, s_res, s_out = (
            sem("o_root"), sem("o_norm"), sem("o_xb"), sem("o_gamma"), sem("o_res"), sem("o_out"))
        STEPS = MOMENT_STEPS + 1
        x_v = ins["x"].rearrange("(n s p) e -> n p s e", s=2, p=P)
        out_v = out.rearrange("(n s p) e -> n p s e", s=2, p=P)
        oT_v = oT_d.rearrange("h p t -> p h t")

        def wide(row):
            return row.unsqueeze(1).to_broadcast([P, 2, E])

        block = ctx.enter_context(nc.Block())

        @block.sync
        def _(sp):
            for c in range(2):
                sp.nop().then_inc(s_o[c], 16)
            for r in range(R):
                sp.nop().then_inc(s_x[r], 16)
                sp.nop().then_inc(s_st[r], 16)

            def store(n, r):
                sp.wait_ge(s_out, 2 * n + 2)
                sp.dma_start(out_v[bass.ds(n, 1)].rearrange("a p s e -> (a p) s e"), acc[r][:, :, :]
                             ).then_inc(s_st[r], 16)

            def body(i, first, last):
                for r in range(R):
                    m = R * i + r
                    if not (last and r >= R - 2):
                        sp.wait_ge(s_olo, m + 1)
                        sp.dma_start(oTs[r % 2][:, :, :], oT_v[:, :, bass.ds((m + 2) * G, G)]
                                     ).then_inc(s_o[r % 2], 16)
                    if not first:
                        store(m - R, r)
                        sp.dma_start(x[r][:, :, :], x_v[bass.ds(m, 1)].rearrange("a p s e -> (a p) s e")
                                     ).then_inc(s_x[r], 16)
            looped(sp, TURNS, body, peel_last=True)
            for r in range(R):
                store(GROUPS - R + r, r)
            for r in range(R):
                sp.wait_ge(s_st[r], 16 * (TURNS + 1))

        @block.gpsimd
        def _(pool):
            nc.gpsimd.memset(ones[:, :], 1.0).then_inc(s_ones, 1)

            def fetch(n):
                r = n % R
                if n >= R:
                    pool.wait_ge(s_out, 2 * (n - R) + 2)
                for s in range(2):
                    c = 2 * n + s
                    pool.indirect_dma_start(
                        out=ff[r][s][:, :], out_offset=None, in_=ys_d,
                        in_offset=bass.IndirectOffsetOnAxis(ap=slot_u[:, c:c + 1], axis=0)
                    ).then_inc(s_ff[r], 16)
                if n == 0:
                    pool.wait_ge(s_scaled, 2)
                pool.wait_ge(s_x[r], 16 * (n // R + 1))
                nc.gpsimd.tensor_tensor(x[r][:, :, :], x[r][:, :, :], wide(beta), ALU.add).then_inc(s_xb, 1)

            fetch(0)
            fetch(1)
            for n in range(GROUPS):
                if n + 2 < GROUPS:
                    fetch(n + 2)
                r = n % R
                pool.wait_ge(s_norm, n + 1)
                nc.gpsimd.tensor_tensor(yn[r][:, :, :], yn[r][:, :, :], wide(gamma), ALU.mult).then_inc(s_gamma, 1)

        @block.scalar
        def _(act):
            def o_high(m, c, half, fresh):
                act.wait_ge(s_o[c], 16 * (half + 1))
                if not fresh:
                    act.wait_ge(s_y, m - 1)
                nc.scalar.copy(op[c][:, 0, :, :], oTs[c][:, :, :]).then_inc(s_ohi, 1)

            act.wait_ge(s_ones, 1)
            nc.scalar.copy(ones_r[:, :], ones[:, :])
            nc.scalar.copy(bop[:, 0, :], rows[0:1, 0, :])
            nc.scalar.copy(wop[:, 0, :, :], wo[:, :, :]).then_inc(s_hi, 1)
            o_high(0, 0, 0, True)
            o_high(1, 1, 0, True)

            def body(i, first, last):
                for a in range(2):
                    q = 2 * i + a
                    if not (last and a == 1):
                        for c in range(2):
                            o_high(2 * q + 2 + c, c, q + 1, False)
                    act.wait_ge(s_d, STEPS * q + RECIPROCAL_STEP)
                    nc.scalar.activation(mom[a][:, 5, :], mom[a][:, 4, :], ACT.Sqrt).then_inc(s_root, 1)
                    act.wait_ge(s_d, STEPS * (q + 1))
                    for c in range(2):
                        r = 2 * a + c
                        if not first:
                            act.wait_ge(s_out, 2 * (2 * q + c - R) + 2)
                        for s in range(2):
                            k = 2 * c + s
                            last_op = nc.scalar.activation(yn[r][:, s, :], p_y[r][:, s, :], ACT.Identity,
                                                           bias=shift[a][:, k:k + 1], scale=mom[a][:, 1, k:k + 1])
                        last_op.then_inc(s_norm, 1)
            looped(act, TURNS, body, peel_last=True)

        @block.tensor
        def _(pe):
            pe.wait_ge(s_lo, 2)

            def body(i, first, last):
                for r in range(R):
                    n, c = R * i + r, r % 2
                    pe.wait_ge(s_olo, n + 1)
                    if not first:
                        pe.wait_ge(s_norm, n - R + 1)
                    for s in range(2):
                        for part in range(2):
                            nc.tensor.matmul(p_y[r][:, s, :], ones_r[:, :], bop[:, part, :],
                                             start=(part == 0), stop=False)
                        for k in range(PAIRS):
                            for t, (e, f) in enumerate(((0, 0), (0, 1), (1, 0))):
                                last_op = nc.tensor.matmul(
                                    p_y[r][:, s, :], op[c][:, e, k, s * P:(s + 1) * P], wop[:, f, k, :],
                                    start=False, stop=(k == PAIRS - 1 and t == 2))
                    last_op.then_inc(s_y, 1)
            looped(pe, TURNS, body)

        @block.vector
        def _(dve):
            v = nc.vector
            v.tensor_scalar(rows[:, 1:3, :], rows[:, 1:3, :], OUT_SCALE, None, ALU.mult).then_inc(s_scaled, 2)
            dve.wait_ge(s_hi, 1)
            v.tensor_tensor(bop[:, 1, :], rows[0:1, 0, :], bop[:, 0, :].bitcast(F32), ALU.subtract).then_inc(s_lo, 1)
            v.tensor_tensor(wop[:, 1, :, :], wo[:, :, :], wop[:, 0, :, :].bitcast(F32), ALU.subtract).then_inc(s_lo, 1)

            def o_low(m, c):
                dve.wait_ge(s_ohi, m + 1)
                v.tensor_tensor(op[c][:, 1, :, :], oTs[c][:, :, :], op[c][:, 0, :, :].bitcast(F32), ALU.subtract
                                ).then_inc(s_olo, 1)

            def combine(n, r, turn):
                dve.wait_ge(s_gamma, n + 1)
                v.tensor_tensor(yn[r][:, :, :], yn[r][:, :, :], x[r][:, :, :], ALU.add).then_inc(s_res, 1)
                dve.wait_ge(s_res, n + 1)
                dve.wait_ge(s_ff[r], 32 * (turn + 1))
                dve.wait_ge(s_st[r], 16 * (turn + 1))
                for s in range(2):
                    v.scalar_tensor_tensor(out=acc[r][:, s, :], in0=ff[r][s][:, :],
                                           scalar=prob[:, bass.ds(2 * n + s, 1)], in1=yn[r][:, s, :],
                                           op0=ALU.mult, op1=ALU.add).then_inc(s_out, 1)

            o_low(0, 0)
            o_low(1, 1)

            def body(i, first, last):
                for a in range(2):
                    q = 2 * i + a
                    for c in range(2):
                        n = 2 * q + c
                        dve.wait_ge(s_y, n + 1)
                        for s in range(2):
                            last_op = v.bn_stats(stats[a][:, 2 * c + s, :], p_y[2 * a + c][:, s, :])
                        last_op.then_inc(s_bn, 1)
                        if not (first and a == 0):
                            before = R * i + c if a == 1 else R * (i - 1) + 2 + c
                            combine(before, 2 * (1 - a) + c, i if a == 1 else i - 1)
                        if not (last and a == 1):
                            o_low(n + 2, c)
                    done = [0]

                    def step(ins_):
                        done[0] += 1
                        ins_.then_inc(s_d, 1)
                        dve.wait_ge(s_d, STEPS * q + done[0])

                    dve.wait_ge(s_bn, 2 * q + 2)
                    moments(nc, dve, step, stats[a], mom[a], s_root, q + 1)
                    v.scalar_tensor_tensor(out=shift[a][:, :], in0=mom[a][:, 0, :], scalar=-1.0, in1=mom[a][:, 1, :],
                                           op0=ALU.mult, op1=ALU.mult).then_inc(s_d, 1)
            looped(dve, TURNS, body, peel_last=True)
            for c in range(2):
                combine(GROUPS - 2 + c, 2 + c, TURNS - 1)


def build(nc, ins, out):
    wp_d = nc.dram_tensor("weight_parts_scratch", [PAIRS, P, 2, WPAIR], F32).ap()
    xn_d = nc.dram_tensor("xn_scratch", [T, E], F32).ap()
    token_d = nc.dram_tensor("token_scratch", [SLOTS, 1], F32).ap()
    ys_d = nc.dram_tensor("ys_scratch", [SLOTS, E], F32).ap()
    oT_d = nc.dram_tensor("oT_scratch", [PAIRS, P, T], F32).ap()
    with ExitStack() as ctx:
        def sb(name, shape, dt=F32):
            return ctx.enter_context(nc.sbuf_tensor(name, shape, dt))

        consts = sb("consts", [P, CONSTS])
        slot_u, prob = sb("slot_u", [P, NT], U32), sb("prob", [P, NT])
        tile_expert = sb("tile_expert", [P, FFN_TILES], I32)
        with ExitStack() as att:
            xT = att.enter_context(nc.sbuf_tensor("xT", [P, KT, T], F32))
            xp = att.enter_context(nc.sbuf_tensor("xp", [P, 2, 2, KT, S], F32R))
            w = [att.enter_context(nc.sbuf_tensor(f"w{j}", [P, 2, WPAIR], F32R)) for j in range(2)]
            with ExitStack() as routing:
                sw = routing.enter_context(nc.sbuf_tensor("sw", [P, KT, NE], F32))
                pL = routing.enter_context(nc.psum_tensor("pL", [P, 512], F32))
                norm_stage(nc, ins, wp_d, xn_d, xT, consts, sw, pL)
                route_stage(nc, ins, wp_d, token_d, xT, xp, w, consts, pL, slot_u, prob, tile_expert)
            attention_stage(nc, ins, wp_d, token_d, oT_d, xT, xp, w, consts, slot_u)
        pre = {"wo": sb("wo", [P, PAIRS, E]),
               "rows": sb("rows", [P, 3, E]),
               "oTs": [sb(f"oTs{c}", [P, PAIRS, 2 * P]) for c in range(2)],
               "x": [sb(f"x{n}", [P, 2, E]) for n in range(4)]}
        ffn_stage(nc, ins, xn_d, token_d, ys_d, oT_d, consts, tile_expert, pre)
        output_stage(nc, ins, oT_d, ys_d, slot_u, prob, pre, out)


def kernel(L0_attn_X, L0_attn_Wq, L0_attn_bq, L0_attn_Wk, L0_attn_bk, L0_attn_Wv, L0_attn_bv, L0_attn_Wo,
           L0_attn_bo, L0_attn_gamma, L0_attn_beta, L0_attn_lam, L0_ffn_switch_w, L0_ffn_switch_b,
           L0_ffn_w1, L0_ffn_b1, L0_ffn_w2, L0_ffn_b2):
    import concourse.bacc as bacc
    import numpy as np
    from concourse.bass_utils import run_bass_kernel_spmd

    def a(x):
        return np.asarray(x)

    def wide(x):
        x = a(x)
        return np.broadcast_to(x[None], (P,) + x.shape)

    def by_pair(wt, width):
        return a(wt).reshape(PAIRS, 2, KT, P, width).transpose(0, 3, 2, 1, 4).reshape(PAIRS, P, KT * 2 * width)

    idx = np.arange(P)
    consts = np.concatenate([
        np.eye(P), idx[:, None] < idx[None, :],
        np.broadcast_to(np.arange(MAXT) * FFN_TILE, (P, MAXT)),
        np.broadcast_to(np.arange(FFN_TILES), (P, FFN_TILES)),
        idx[:, None] + P * np.arange(NT)[None]], axis=1).astype(np.float32)
    arrays = {
        "x": a(L0_attn_X).reshape(T, E),
        "consts": consts,
        "sw": a(L0_ffn_switch_w).reshape(KT, P, NE).transpose(1, 0, 2),
        "swb": wide(L0_ffn_switch_b),
        "w_attn": np.concatenate([by_pair(L0_attn_Wq, 2 * D), by_pair(L0_attn_Wk, 2 * D),
                                  by_pair(L0_attn_Wv, D)], axis=2),
        "attn_bias": np.concatenate([a(L0_attn_bq).T.reshape(P, PAIRS, 2), a(L0_attn_bk).T.reshape(P, PAIRS, 2),
                                     a(L0_attn_bv).reshape(PAIRS, P).T[:, :, None]], axis=2),
        "lam": np.broadcast_to(a(L0_attn_lam).reshape(1, 1), (P, 1)),
        "w1": a(L0_ffn_w1).reshape(NE, KT, P, F).transpose(0, 2, 1, 3),
        "w2": a(L0_ffn_w2).reshape(NE, FT, P, E).transpose(0, 2, 1, 3),
        "b1": a(L0_ffn_b1).reshape(NE, FT, P).transpose(0, 2, 1),
        "b2": np.broadcast_to(a(L0_ffn_b2)[:, None, :], (NE, P, E)),
        "wo": a(L0_attn_Wo).reshape(PAIRS, P, E).transpose(1, 0, 2),
        "out_rows": np.stack([wide(L0_attn_bo), wide(L0_attn_gamma), wide(L0_attn_beta)], axis=1),
    }
    arrays = {k: np.ascontiguousarray(x) for k, x in arrays.items()}
    nc = bacc.Bacc("TRN2", target_bir_lowering=False, num_devices=1)
    ins = {k: nc.dram_tensor("in_" + k, x.shape, F32, kind="ExternalInput").ap() for k, x in arrays.items()}
    out = nc.dram_tensor("out", [T, E], F32, kind="ExternalOutput").ap()
    build(nc, ins, out)
    r = run_bass_kernel_spmd(nc, [{"in_" + k: x for k, x in arrays.items()}], core_ids=[0])
    return r.results[0]["out"].reshape(B, S, E)
```
